# Optimizing a Trainium2 kernel written in Bass

```python
import numpy as np
import jax
import jax.numpy as jnp

def _softmax(x, axis=-1):
    return jax.nn.softmax(x, axis=axis)

def _gelu(x):
    return jax.nn.gelu(x, approximate=True)

def _silu(x):
    return jax.nn.silu(x)

def _sigmoid(x):
    return jax.nn.sigmoid(x)

def _layernorm(x, axis=-1, eps=1e-05):
    m = jnp.mean(x, axis=axis, keepdims=True)
    v = jnp.var(x, axis=axis, keepdims=True)
    return (x - m) / jnp.sqrt(v + eps)

def _scatter_add(tgt, idx, src, axis=0):
    return tgt.at[idx].add(src)

def _segment_sum(src, seg, n):
    return jax.ops.segment_sum(src, seg, n)
kernel_name = 'mk_gnn_preln_d1_gnn_r8_056af2'

def setup_inputs(seed: int=0):
    np.random.seed(seed)
    _w = jnp.asarray

    def _rec_inputs():
        import jax
        import jax.numpy as jnp
        _gk = jax.random.key(seed)
        x = -0.000202 + 1 * jax.random.normal(jax.random.fold_in(_gk, 1), (6250, 128), jnp.float32)
        _s = jax.random.randint(jax.random.fold_in(_gk, 2), (50000,), 0, 6250, jnp.int32)
        _d = jax.random.randint(jax.random.fold_in(_gk, 3), (50000,), 0, 6250, jnp.int32)
        _loop = jnp.arange(6250, dtype=jnp.int32)
        src = jnp.concatenate([_s, _d, _loop])
        dst = jnp.concatenate([_d, _s, _loop])
        _o = jnp.argsort(dst, stable=True)
        src = src[_o]
        dst = dst[_o]
        edge_attr_128 = -8.16379e-05 + 0.999858 * jax.random.normal(jax.random.fold_in(_gk, 12), (106250, 128), jnp.float32)
        return (x, src, dst, edge_attr_128)
    x, src, dst, edge_attr_128 = _rec_inputs()

    def _L0_gnn_setup():
        import jax, jax.numpy as jnp
        import numpy as np
        N_NODES = 6250
        N_EDGES = 100000
        NODE_DIM = 128
        EDGE_DIM = 128
        OUT_FEATS = 128
        key = jax.random.key(seed)
        k1, k2, k3, k4, k5, k6 = jax.random.split(key, 6)
        node_features = jax.random.normal(k1, (N_NODES, NODE_DIM), dtype=jnp.float32)
        edge_features = jax.random.normal(k2, (N_EDGES, EDGE_DIM), dtype=jnp.float32)
        src = jax.random.randint(k3, (N_EDGES,), 0, N_NODES, dtype=jnp.int32)
        dst = jax.random.randint(k4, (N_EDGES,), 0, N_NODES, dtype=jnp.int32)
        in_dim = 2 * NODE_DIM + EDGE_DIM
        W = jax.random.normal(k5, (OUT_FEATS, in_dim), dtype=jnp.float32) / np.sqrt(in_dim)
        b = jax.random.normal(k6, (OUT_FEATS,), dtype=jnp.float32) * 0.01
        return {'node_features': node_features, 'edge_features': edge_features, 'src': src, 'dst': dst, 'W': W, 'b': b}
    _L0_gnn_all = _L0_gnn_setup()
    _L0_gnn_in = {k: v for k, v in _L0_gnn_all.items() if k in ('W', 'b')}
    del _L0_gnn_all
    return {'x': x, 'src': src, 'dst': dst, 'edge_attr_128': edge_attr_128, 'L0_gnn_W': _L0_gnn_in['W'], 'L0_gnn_b': _L0_gnn_in['b']}

def reference(x, src, dst, edge_attr_128, L0_gnn_W, L0_gnn_b):
    import jax
    import jax.numpy as jnp

    def _L0_gnn_ref(node_features, edge_features, src, dst, W, b):
        import jax, jax.numpy as jnp
        import numpy as np
        N_NODES = 6250
        N_EDGES = 100000
        NODE_DIM = 128
        EDGE_DIM = 128
        OUT_FEATS = 128
        agg_src = jax.ops.segment_sum(node_features[src], dst, num_segments=N_NODES)
        agg_edge = jax.ops.segment_sum(edge_features, dst, num_segments=N_NODES)
        h = jnp.concatenate([node_features, agg_src, agg_edge], axis=1)
        h = h @ W.T + b
        return jax.nn.relu(h)
    h = jnp.maximum(_layernorm(x, axis=-1), 0.0)
    x = x + _L0_gnn_ref(h, edge_attr_128, src, dst, L0_gnn_W, L0_gnn_b)
    return x

_drawn_inputs = setup_inputs


def setup_inputs(seed=0):
    import zlib

    import numpy as np

    out = dict(_drawn_inputs(seed))
    spreads = {}
    factors = {'L0_gnn_b': 27.172}
    for name, (base, spread) in spreads.items():
        noise = np.random.default_rng([zlib.crc32(name.encode()), seed]).standard_normal(out[name].shape)
        drawn = base * np.exp(spread * noise) if base else spread * noise
        out[name] = jnp.asarray(drawn.astype(out[name].dtype))
    for name, factor in factors.items():
        out[name] = (out[name] * factor).astype(out[name].dtype)
    return out
```

```python
import numpy as np
import concourse.bass as bass
import concourse.mybir as mybir
from concourse.alu_op_type import AluOpType as ALU
from contextlib import ExitStack

F32 = mybir.dt.float32
I32 = mybir.dt.int32
ACT = mybir.ActivationFunctionType
AX = mybir.AxisListType.X
P = 128
EPS = 1e-5


def build(nc, x, src, dst, edge_attr, w, b, out):
    nodes, feats = x.shape
    edges = src.shape[0]
    assert feats == P
    K = 5
    BATCH = K * P
    FULL = edges // BATCH
    TAIL = edges - FULL * BATCH
    TAIL_P = TAIL // K
    assert TAIL and TAIL % K == 0 and TAIL_P >= 2 and FULL % 2 == 0
    NB = FULL + 1
    ROWS2 = NB - P
    WIN = 48
    TILES = -(-nodes // P)
    LAST = nodes - (TILES - 1) * P
    CT = 7
    CHUNKS = TILES // CT
    assert TILES == CHUNKS * CT
    WIDE = 512
    NWIDE = -(-nodes // WIDE)
    AGG = max(NWIDE * WIDE, nodes + WIN, TILES * P)

    ctx = ExitStack()
    with ctx:
        def sb(name, shape, dt=F32):
            return ctx.enter_context(nc.sbuf_tensor(name, shape, dt))

        def pb(name):
            return ctx.enter_context(nc.psum_tensor(name, [P, 512], F32))

        def sem(name):
            return ctx.enter_context(nc.semaphore(name))

        h_dram = nc.dram_tensor("h_dram", [nodes, feats], F32, kind="Internal").ap()

        x_sb = sb("x_sb", [P, TILES, P])
        h_sb = sb("h_sb", [P, TILES, P])
        hT = sb("hT", [P, TILES * P])
        agg = sb("agg", [P, 2, AGG])
        w_sb = sb("w_sb", [P, 3, P])
        wT = sb("wT", [P, 3, P])
        b_row = sb("b_row", [1, P])
        ones = sb("ones", [P, P])
        ident = sb("ident", [P, P])
        iota_i = sb("iota_i", [P, WIDE], I32)
        iota = sb("iota", [P, WIDE])
        eps = sb("eps", [P, 1])
        stats = sb("stats", [P, CT, 6])
        mv = sb("mv", [P, TILES, 2])
        std = sb("std", [P, TILES])
        rstd = sb("rstd", [P, TILES])
        rows_i = sb("rows_i", [P, 4, BATCH], I32)
        rows = sb("rows", [P, 4, BATCH])
        lo = sb("lo", [P, 2])
        hi = sb("hi", [P, 2])
        wide_span = sb("wide_span", [P, 2])
        diag = sb("diag", [P, 2, P])
        base = sb("base", [P, NB])
        base_i = sb("base_i", [1, NB], I32)
        flag_i = sb("flag_i", [1, 1], I32)
        idx = sb("idx", [P, K, NB], I32)
        rel = sb("rel", [P, K, NB])
        idx_now = sb("idx_now", [P, 2, K], I32)
        onehot = sb("onehot", [P, 2, K, WIN])
        gathered = sb("gathered", [P, 2, K, P])
        edge_rows = sb("edge_rows", [P, 2, K, P])
        left = sb("left", [P, K])
        in_win = sb("in_win", [P, K])
        left_rel = sb("left_rel", [P, K])
        wide_hot = sb("wide_hot", [P, K, WIDE])
        z = sb("z", [P, 512])

        acc = [pb(f"acc{s}") for s in range(2)]
        wideE, wideS = pb("wideE"), pb("wideS")
        half = [pb("halfA"), pb("halfB")]
        tr = [pb("trA"), pb("trB")]
        HALVES = [(0, 4), (4, CT)]

        s_x = [sem(f"x_loaded{c}") for c in range(CHUNKS)]
        s_w = sem("weights_loaded")
        s_rows = sem("rows_loaded")
        s_const = sem("consts_ready")
        s_zero = sem("zeroed")
        s_iota = sem("iota_ready")
        s_xpad = sem("x_pad_zeroed")
        s_dve = sem("dve_step")
        s_var = sem("variance_ready")
        s_std = sem("std_ready")
        s_norm = sem("norm_ready")
        s_h = sem("h_ready")
        s_hstored = sem("h_stored")
        s_rowsf = sem("rows_as_float")
        s_diag = sem("diag_ready")
        s_base = sem("base_ready")
        s_tr = sem("transposed")
        s_trc = sem("transposed_copied")
        s_hT = sem("hT_half_ready")
        s_hTc = sem("hT_half_copied")
        s_wTp = sem("wT_transposed")
        s_wT = sem("wT_ready")
        s_go = sem("gathers_may_go")
        s_idx = sem("idx_staged")
        s_gath = [sem(f"gathered{s}") for s in range(2)]
        s_edge = [sem(f"edges_loaded{s}") for s in range(2)]
        s_edge_used = [sem(f"edges_used{s}") for s in range(2)]
        s_acc = [sem(f"window_summed{s}") for s in range(2)]
        s_added = [sem(f"window_added{s}") for s in range(2)]
        s_hot = [sem(f"onehot_ready{s}") for s in range(2)]
        s_gidx = sem("general_idx_staged")
        s_gg = sem("general_gathered")
        s_ge = sem("general_edges")
        s_gl = sem("general_left")
        s_gh = sem("general_onehot")
        s_gm = sem("general_summed")
        s_ga = sem("general_added")
        s_fp = sem("final_product")
        s_fo = [sem(f"final_done{a}") for a in range(2)]
        s_out = sem("out_stored")

        def node_tiles(a, t0, t1):
            return a[t0 * P:t1 * P, :].rearrange("(t p) f -> p t f", p=P)

        edge_full = edge_attr[0:FULL * BATCH, :].rearrange("(n p k) f -> p n (k f)", p=P, k=K)
        edge_tail = edge_attr[FULL * BATCH:edges, :].rearrange("(p k) f -> p (k f)", k=K)

        block = ctx.enter_context(nc.Block())


        @block.sync
        def _(sp):
            for a, v in ((0, src), (2, dst)):
                sp.dma_start(rows_i[:, a, :], v[0:P * BATCH].rearrange("(n e) -> n e", e=BATCH)).then_inc(s_rows, 16)
                sp.dma_start(rows_i[0:ROWS2 - 1, a + 1, :],
                             v[P * BATCH:FULL * BATCH].rearrange("(n e) -> n e", e=BATCH)).then_inc(s_rows, 16)
                sp.dma_start(rows_i[ROWS2 - 1:ROWS2, a + 1, 0:TAIL],
                             v[FULL * BATCH:edges].rearrange("(n e) -> n e", n=1)).then_inc(s_rows, 16)
                sp.dma_start(rows_i[ROWS2 - 1:ROWS2, a + 1, TAIL:BATCH],
                             v[(FULL - 1) * BATCH + TAIL:FULL * BATCH].rearrange("(n e) -> n e", n=1)).then_inc(s_rows, 16)
            for c in range(CHUNKS):
                sp.wait_ge(s_h, c + 1)
                full = CT if c < CHUNKS - 1 else CT - 1
                sp.dma_start(node_tiles(h_dram, c * CT, c * CT + full),
                             h_sb[:, c * CT:c * CT + full, :]).then_inc(s_hstored, 16)
            sp.dma_start(h_dram[(TILES - 1) * P:nodes, :], h_sb[0:LAST, TILES - 1, :]).then_inc(s_hstored, 16)
            with sp.Fori(0, FULL // 2) as i:
                for s in range(2):
                    sp.wait_ge(s_edge_used[s], i + 1)
                    sp.dma_start(edge_rows[:, s, :, :].rearrange("p k f -> p (k f)"),
                                 edge_full[:, bass.ds(2 * i + s, 1), :].rearrange("p o e -> p (o e)")).then_inc(s_edge[s], 16)
            sp.wait_ge(s_edge_used[0], FULL // 2 + 1)
            sp.dma_start(edge_rows[0:TAIL_P, 0, :, :].rearrange("p k f -> p (k f)"), edge_tail).then_inc(s_edge[0], 16)

            sp.wait_ge(s_added[0], FULL // 2 + 2)
            flag = sp.value_load(flag_i[0:1, 0:1], min_val=0, max_val=1)
            with sp.If(flag != 0):
                with sp.Fori(0, FULL) as n:
                    sp.wait_ge(s_ga, n * NWIDE + 1)
                    sp.dma_start(edge_rows[:, 0, :, :].rearrange("p k f -> p (k f)"),
                                 edge_full[:, bass.ds(n, 1), :].rearrange("p o e -> p (o e)")).then_inc(s_ge, 16)
                sp.wait_ge(s_ga, FULL * NWIDE + 1)
                sp.dma_start(edge_rows[0:TAIL_P, 0, :, :].rearrange("p k f -> p (k f)"), edge_tail).then_inc(s_ge, 16)

            for c in range(CHUNKS):
                for a in range(2):
                    sp.wait_ge(s_fo[a], c + 1)
                full = CT if c < CHUNKS - 1 else CT - 1
                sp.dma_start(node_tiles(out, c * CT, c * CT + full),
                             h_sb[:, c * CT:c * CT + full, :]).then_inc(s_out, 16)
            sp.dma_start(out[(TILES - 1) * P:nodes, :], h_sb[0:LAST, TILES - 1, :]).then_inc(s_out, 16)
            sp.wait_ge(s_out, 16 * (CHUNKS + 1))

        @block.gpsimd
        def _(pool):
            pool.memset(ident[:, :], 0.0).then_inc(s_zero, 1)
            pool.memset(ones[:, :], 1.0).then_inc(s_const, 1)
            pool.wait_ge(s_zero, 1)
            pool.affine_select(out=ident[:, :], in_=ident[:, :], compare_op=ALU.not_equal, fill=1.0, base=0,
                               pattern=[[-1, P]], channel_multiplier=1).then_inc(s_const, 1)
            pool.iota(iota_i[:, :], pattern=[[1, WIDE]], base=0, channel_multiplier=0).then_inc(s_iota, 1)
            pool.memset(agg[:, :, :], 0.0).then_inc(s_const, 1)

            def gather(slot, rows_, k, done):
                pool.indirect_dma_start(out=gathered[0:rows_, slot, k, :], out_offset=None, in_=h_dram,
                                        in_offset=bass.IndirectOffsetOnAxis(ap=idx_now[0:rows_, slot, k:k + 1], axis=0)
                                        ).then_inc(done, 16)

            pool.wait_ge(s_hstored, 16 * (CHUNKS + 1))
            with pool.Fori(0, FULL // 2) as i:
                for s in range(2):
                    pool.wait_ge(s_idx, 2 * i + s + 1)
                    pool.wait_ge(s_acc[s], i + 1)
                    pool.sem_inc(s_go, 1)
                    for k in range(K):
                        gather(s, P, k, s_gath[s])
            pool.wait_ge(s_idx, NB)
            pool.wait_ge(s_acc[0], FULL // 2 + 1)
            for k in range(K):
                gather(0, TAIL_P, k, s_gath[0])

            pool.wait_ge(s_added[0], FULL // 2 + 2)
            flag = pool.value_load(flag_i[0:1, 0:1], min_val=0, max_val=1)
            with pool.If(flag != 0):
                with pool.Fori(0, FULL) as n:
                    pool.wait_ge(s_gidx, n + 1)
                    pool.sem_inc(s_go, 1)
                    for k in range(K):
                        gather(0, P, k, s_gg)
                pool.wait_ge(s_gidx, NB)
                for k in range(K):
                    gather(0, TAIL_P, k, s_gg)

        @block.scalar
        def _(act):
            for c in range(CHUNKS):
                full = CT if c < CHUNKS - 1 else CT - 1
                if c == CHUNKS - 1:
                    act.wait_ge(s_xpad, 1)
                    act.dma_start(x_sb[0:LAST, TILES - 1, :], x[(TILES - 1) * P:nodes, :]).then_inc(s_x[c], 16)
                act.dma_start(x_sb[:, c * CT:c * CT + full, :], node_tiles(x, c * CT, c * CT + full)).then_inc(s_x[c], 16)
            act.dma_start(w_sb[:, :, :].rearrange("o c f -> o (c f)"), w).then_inc(s_w, 16)
            act.dma_start(b_row[0:1, :], b.rearrange("(o f) -> o f", o=1)).then_inc(s_w, 16)

            for c in range(CHUNKS):
                t = slice(c * CT, (c + 1) * CT)
                act.wait_ge(s_var, c + 1)
                nc.scalar.activation(std[:, t], mv[:, t, 1], ACT.Sqrt, bias=eps[:, :]).then_inc(s_std, 1)
                act.wait_ge(s_norm, c + 1)
                nc.scalar.activation(h_sb[:, t, :], h_sb[:, t, :], ACT.Relu).then_inc(s_h, 1)
            act.wait_ge(s_trc, 3)

            def stage(n, s):
                nc.scalar.copy(idx_now[:, s, :], idx[:, :, bass.ds(n, 1)].rearrange("p k o -> p (k o)")).then_inc(s_idx, 1)

            for s in range(2):
                stage(s, s)
            act.wait_ge(s_wTp, 1)
            nc.scalar.copy(wT[:, :, :].rearrange("f c o -> f (c o)"), tr[0][:, 0:3 * P]).then_inc(s_wT, 1)
            for c in range(CHUNKS):
                for a, (t0, t1) in enumerate(HALVES):
                    act.wait_ge(s_hT, 2 * c + a + 1)
                    nc.scalar.copy(hT[:, (c * CT + t0) * P:(c * CT + t1) * P],
                                   half[a][:, 0:(t1 - t0) * P]).then_inc(s_hTc, 1)
            with act.Fori(1, FULL // 2) as i:
                for s in range(2):
                    act.wait_ge(s_acc[s], i + 1)
                    stage(2 * i + s, s)
            act.wait_ge(s_acc[0], FULL // 2 + 1)
            stage(FULL, 0)

            act.wait_ge(s_added[0], FULL // 2 + 2)
            flag = act.value_load(flag_i[0:1, 0:1], min_val=0, max_val=1)
            with act.If(flag != 0):
                with act.Fori(0, NB) as n:
                    act.wait_ge(s_ga, n * NWIDE + 1)
                    nc.scalar.copy(idx_now[:, 0, :], idx[:, :, bass.ds(n, 1)].rearrange("p k o -> p (k o)")).then_inc(s_gidx, 1)

        @block.vector
        def _(dve):
            steps = [0]
            for given in (*s_added, s_ga):
                dve.sem_inc(given, 1)

            def then(ins):
                steps[0] += 1
                ins.then_inc(s_dve, 1)
                dve.wait_ge(s_dve, steps[0])

            nc.vector.memset(x_sb[:, TILES - 1, :], 0.0).then_inc(s_xpad, 1)
            then(nc.vector.memset(eps[:, :], EPS))
            for c in range(CHUNKS):
                t0 = c * CT
                dve.wait_ge(s_x[c], 16 if c < CHUNKS - 1 else 32)
                for t in range(CT):
                    last = nc.vector.bn_stats(stats[:, t, :], x_sb[:, t0 + t, :])
                then(last)
                for t in range(CT):
                    last = nc.vector.bn_aggr(mv[:, t0 + t, :], stats[:, t, :])
                last.then_inc(s_var, 1)
                dve.wait_ge(s_std, c + 1)
                then(nc.vector.reciprocal(rstd[:, t0:t0 + CT], std[:, t0:t0 + CT]))
                for t in range(t0, t0 + CT):
                    last = nc.vector.tensor_scalar(h_sb[:, t, :], x_sb[:, t, :], mv[:, t, 0:1], rstd[:, t:t + 1],
                                                   ALU.subtract, ALU.mult)
                last.then_inc(s_norm, 1)

            dve.wait_ge(s_rows, 16 * 8)
            nr = (P, ROWS2)
            for a in (2, 3, 0, 1):
                last = nc.vector.tensor_copy(rows[0:nr[a % 2], a, :], rows_i[0:nr[a % 2], a, :])
            last.then_inc(s_rowsf, 1)
            dve.wait_ge(s_rowsf, 1)
            for a in range(2):
                nc.vector.tensor_reduce(lo[0:nr[a], a:a + 1], rows[0:nr[a], 2 + a, :], AX, ALU.min)
                last = nc.vector.tensor_reduce(hi[0:nr[a], a:a + 1], rows[0:nr[a], 2 + a, :], AX, ALU.max)
            then(last)
            dve.wait_ge(s_const, 3)
            for a in range(2):
                nc.vector.tensor_scalar(diag[0:nr[a], a, 0:nr[a]], ident[0:nr[a], 0:nr[a]], lo[0:nr[a], a:a + 1], None,
                                        ALU.mult)
                last = nc.vector.tensor_tensor(hi[0:nr[a], a:a + 1], hi[0:nr[a], a:a + 1], lo[0:nr[a], a:a + 1],
                                               ALU.subtract)
            then(last)
            for a in range(2):
                last = nc.vector.tensor_scalar(wide_span[0:nr[a], a:a + 1], hi[0:nr[a], a:a + 1], float(WIN), None, ALU.is_ge)
            last.then_inc(s_diag, 1)
            dve.wait_ge(s_iota, 1)
            nc.vector.tensor_copy(iota[:, :], iota_i[:, :])
            dve.wait_ge(s_base, 1)
            nc.vector.tensor_copy(base[:, :], half[0][:, 0:NB])
            nc.vector.tensor_copy(base_i[0:1, :], half[0][0:1, 0:NB])
            then(nc.vector.tensor_scalar(flag_i[0:1, 0:1], half[0][0:1, NB:NB + 1], 1.0, None, ALU.min))
            for k0, k1 in ((0, 3), (3, K)):
                n = k1 - k0
                dve.wait_ge(s_tr, 2 * (k0 // 3) + 1)
                nc.vector.tensor_copy(idx[:, k0:k1, :], tr[0][:, 0:n * NB].rearrange("p (k n) -> p k n", k=n)
                                      ).then_inc(s_trc, 1)
                dve.wait_ge(s_tr, 2 * (k0 // 3) + 2)
                last = nc.vector.tensor_tensor(rel[:, k0:k1, :], tr[1][:, 0:n * NB].rearrange("p (k n) -> p k n", k=n),
                                               base[:, :].unsqueeze(1).broadcast_to([P, n, NB]), ALU.subtract)
                last.then_inc(s_trc, 1)
            dve.wait_ge(s_trc, 4)

            def make_onehot(n, s):
                nc.vector.tensor_tensor(onehot[:, s, :, :],
                                        rel[:, :, bass.ds(n, 1)].broadcast_to([P, K, WIN]),
                                        iota[:, 0:WIN].unsqueeze(1).broadcast_to([P, K, WIN]),
                                        ALU.is_equal).then_inc(s_hot[s], 1)

            def add_window(n, s, others):
                first = dve.value_load(base_i[0:1, bass.ds(n, 1)], min_val=0, max_val=nodes - 1)
                dve.wait_ge(s_added[1 - s], others)
                nc.vector.tensor_tensor(agg[:, :, bass.ds(first, WIN)], agg[:, :, bass.ds(first, WIN)],
                                        acc[s][:, 0:2 * WIN].rearrange("p (a w) -> p a w", a=2),
                                        ALU.add).then_inc(s_added[s], 1)

            make_onehot(0, 0)
            with dve.Fori(0, FULL // 2) as i:
                dve.wait_ge(s_acc[1], i + 1)
                make_onehot(2 * i + 1, 1)
                dve.wait_ge(s_acc[0], i + 2)
                add_window(2 * i, 0, i + 1)
                make_onehot(2 * i + 2, 0)
                dve.wait_ge(s_acc[1], i + 2)
                add_window(2 * i + 1, 1, i + 2)
            dve.wait_ge(s_acc[0], FULL // 2 + 2)
            add_window(FULL, 0, FULL // 2 + 1)

            dve.wait_ge(s_added[0], FULL // 2 + 2)
            flag = dve.value_load(flag_i[0:1, 0:1], min_val=0, max_val=1)
            with dve.If(flag != 0):
                with dve.Fori(0, NB) as n:
                    dve.wait_ge(s_ga, n * NWIDE + 1)
                    r = rel[:, :, bass.ds(n, 1)].rearrange("p k o -> p (k o)")
                    nc.vector.tensor_scalar(in_win[:, :], r, float(WIN), None, ALU.is_ge)
                    nc.vector.tensor_scalar(left[:, :], r, base[:, bass.ds(n, 1)], 1.0, ALU.add, ALU.add).then_inc(s_gl, 1)
                    dve.wait_ge(s_gl, 3 * n + 1)
                    nc.vector.tensor_tensor(left[:, :], left[:, :], in_win[:, :], ALU.mult).then_inc(s_gl, 1)
                    dve.wait_ge(s_gl, 3 * n + 2)
                    nc.vector.tensor_scalar(left[:, :], left[:, :], -1.0, None, ALU.add).then_inc(s_gl, 1)
                    with dve.Fori(0, NWIDE) as j:
                        dve.wait_ge(s_gl, 3 * n + 3)
                        nc.vector.tensor_tensor(wide_hot[:, :, :],
                                                left[:, :].unsqueeze(2).broadcast_to([P, K, WIDE]),
                                                iota[:, :].unsqueeze(1).broadcast_to([P, K, WIDE]),
                                                ALU.is_equal).then_inc(s_gh, 1)
                        dve.wait_ge(s_gh, (n * NWIDE + j + 1))
                        nc.vector.tensor_scalar(left[:, :], left[:, :], -float(WIDE), None, ALU.add)
                        dve.wait_ge(s_gm, n * NWIDE + j + 1)
                        nc.vector.tensor_tensor(agg[:, 0, bass.ds(j * WIDE, WIDE)], agg[:, 0, bass.ds(j * WIDE, WIDE)],
                                                wideE[:, :], ALU.add)
                        nc.vector.tensor_tensor(agg[:, 1, bass.ds(j * WIDE, WIDE)], agg[:, 1, bass.ds(j * WIDE, WIDE)],
                                                wideS[:, :], ALU.add).then_inc(s_ga, 1)
                        dve.wait_ge(s_ga, n * NWIDE + j + 2)

            with dve.Fori(0, CHUNKS) as c:
                for a, (t0, t1) in enumerate(HALVES):
                    n = (t1 - t0) * P
                    dve.wait_ge(s_fp, 2 * c + a + 1)
                    nc.vector.scalar_tensor_tensor(
                        out=h_sb[:, bass.ds(CT * c + t0, t1 - t0), :].rearrange("p t f -> p (t f)"),
                        in0=half[a][:, 0:n], scalar=0.0,
                        in1=x_sb[:, bass.ds(CT * c + t0, t1 - t0), :].rearrange("p t f -> p (t f)"),
                        op0=ALU.max, op1=ALU.add).then_inc(s_fo[a], 1)

        @block.tensor
        def _(pe):
            for given in (*s_edge_used, *s_acc):
                pe.sem_inc(given, 1)
            nr = (P, ROWS2)
            pe.wait_ge(s_diag, 1)
            pe.wait_ge(s_const, 3)
            for a in range(2):
                nc.tensor.matmul(half[0][:, a * P:a * P + nr[a]], ones[0:nr[a], :], diag[0:nr[a], a, 0:nr[a]],
                                 start=True, stop=True)
            nc.tensor.matmul(half[0][:, NB:NB + 1], ones[:, :], wide_span[:, 0:1], start=True, stop=False)
            nc.tensor.matmul(half[0][:, NB:NB + 1], ones[0:ROWS2, :], wide_span[0:ROWS2, 1:2], start=False,
                             stop=True).then_inc(s_base, 1)
            for k0, k1 in ((0, 3), (3, K)):
                for v in range(2):
                    if k0:
                        pe.wait_ge(s_trc, v + 1)
                    for k in range(k0, k1):
                        for a in range(2):
                            c0 = (k - k0) * NB + a * P
                            last = nc.tensor.transpose(
                                tr[v][:, c0:c0 + nr[a]],
                                rows[0:nr[a], 2 * v + a, :].rearrange("n (p k) -> n k p", k=K)[:, k, :],
                                ident[0:nr[a], 0:nr[a]])
                    last.then_inc(s_tr, 1)
            pe.wait_ge(s_w, 32)
            pe.wait_ge(s_trc, 4)
            for c in range(3):
                last = nc.tensor.transpose(tr[0][:, c * P:(c + 1) * P], w_sb[:, c, :], ident[:, :])
            last.then_inc(s_wTp, 1)
            for c in range(CHUNKS):
                pe.wait_ge(s_h, c + 1)
                for a, (t0, t1) in enumerate(HALVES):
                    if c:
                        pe.wait_ge(s_hTc, 2 * c + a - 1)
                    for t in range(t0, t1):
                        last = nc.tensor.transpose(half[a][:, (t - t0) * P:(t - t0 + 1) * P], h_sb[:, c * CT + t, :],
                                                   ident[:, :])
                    last.then_inc(s_hT, 1)

            def products(s, rows_, hot, edges_in, used, gath_in, done):
                pe.wait_ge(*edges_in)
                pe.wait_ge(*hot)
                for k in range(K):
                    last = nc.tensor.matmul(acc[s][:, 0:WIN], edge_rows[0:rows_, s, k, :], onehot[0:rows_, s, k, :],
                                            start=(k == 0), stop=(k == K - 1))
                last.then_inc(used, 1)
                pe.wait_ge(*gath_in)
                for k in range(K):
                    last = nc.tensor.matmul(acc[s][:, WIN:2 * WIN], gathered[0:rows_, s, k, :], onehot[0:rows_, s, k, :],
                                            start=(k == 0), stop=(k == K - 1))
                last.then_inc(done, 1)

            with pe.Fori(0, FULL // 2) as i:
                for s in range(2):
                    pe.wait_ge(s_added[s], i + 1)
                    products(s, P, (s_hot[s], i + 1), (s_edge[s], 16 * i + 16), s_edge_used[s],
                             (s_gath[s], 16 * K * (i + 1)), s_acc[s])
            pe.wait_ge(s_added[0], FULL // 2 + 1)
            products(0, TAIL_P, (s_hot[0], FULL // 2 + 1), (s_edge[0], 16 * (FULL // 2 + 1)), s_edge_used[0],
                     (s_gath[0], 16 * K * (FULL // 2 + 1)), s_acc[0])

            pe.wait_ge(s_added[0], FULL // 2 + 2)
            flag = pe.value_load(flag_i[0:1, 0:1], min_val=0, max_val=1)
            with pe.If(flag != 0):
                def wide_products(rows_, done):
                    pe.wait_ge(s_gh, done + 1)
                    pe.wait_ge(s_ga, done + 1)
                    for o, v in ((wideE, edge_rows), (wideS, gathered)):
                        for k in range(K):
                            last = nc.tensor.matmul(o[:, :], v[0:rows_, 0, k, :], wide_hot[0:rows_, k, :],
                                                    start=(k == 0), stop=(k == K - 1))
                    last.then_inc(s_gm, 1)

                with pe.Fori(0, FULL) as n:
                    with pe.Fori(0, NWIDE) as j:
                        pe.wait_ge(s_ge, 16 * n + 16)
                        pe.wait_ge(s_gg, 16 * K * n + 16 * K)
                        wide_products(P, n * NWIDE + j)
                pe.wait_ge(s_ge, 16 * NB)
                pe.wait_ge(s_gg, 16 * K * NB)
                with pe.Fori(0, NWIDE) as j:
                    wide_products(TAIL_P, FULL * NWIDE + j)
                pe.wait_ge(s_ga, NB * NWIDE + 1)

            pe.wait_ge(s_wT, 1)
            pe.wait_ge(s_hTc, 2 * CHUNKS)
            for c in range(CHUNKS):
                for a, (t0, t1) in enumerate(HALVES):
                    if c:
                        pe.wait_ge(s_fo[a], c)
                    for t in range(t0, t1):
                        o = half[a][:, (t - t0) * P:(t - t0 + 1) * P]
                        n = slice((c * CT + t) * P, (c * CT + t + 1) * P)
                        nc.tensor.matmul(o, ones[0:1, :], b_row[0:1, :], start=True, stop=False)
                        nc.tensor.matmul(o, hT[:, n], wT[:, 0, :], start=False, stop=False)
                        nc.tensor.matmul(o, agg[:, 1, n], wT[:, 1, :], start=False, stop=False)
                        last = nc.tensor.matmul(o, agg[:, 0, n], wT[:, 2, :], start=False, stop=True)
                    last.then_inc(s_fp, 1)


_INS = ["x", "src", "dst", "edge_attr_128", "L0_gnn_W", "L0_gnn_b"]


def kernel(**inputs):
    import concourse.bacc as bacc
    from concourse.bass_utils import run_bass_kernel_spmd

    nc = bacc.Bacc("TRN2", target_bir_lowering=False, num_devices=1)
    arrays, args = {}, []
    for name in _INS:
        a = np.ascontiguousarray(inputs[name])
        arrays[f"in_{name}"] = a
        args.append(nc.dram_tensor(f"in_{name}", a.shape, mybir.dt.from_np(a.dtype), kind="ExternalInput").ap())
    shape = inputs["x"].shape
    args.append(nc.dram_tensor("result", shape, F32, kind="ExternalOutput").ap())
    build(nc, *args)
    r = run_bass_kernel_spmd(nc, [arrays], core_ids=[0])
    return r.results[0]["result"]
```

```python
import numpy as np
import concourse.bass as bass
import concourse.mybir as mybir
from concourse.alu_op_type import AluOpType as ALU
from contextlib import ExitStack

F32 = mybir.dt.float32
F16 = mybir.dt.float16
BF16 = mybir.dt.bfloat16
I32 = mybir.dt.int32
ACT = mybir.ActivationFunctionType
AX = mybir.AxisListType.X
P = 128
EPS = 1e-5
LO_SCALE = 2.0 ** 11


def build(nc, x, src, dst, edge_attr, w, b, out):
    nodes, feats = x.shape
    edges = src.shape[0]
    assert feats == P
    K = 5
    BATCH = K * P
    FULL = edges // BATCH
    TAIL = edges - FULL * BATCH
    assert 2 <= TAIL <= P and FULL % 2 == 0
    HALF = FULL // 2
    NB = FULL + 1
    ROWS2 = NB - P
    WIN = 48
    NG_ = 4
    NSEL = 4
    TILES = -(-nodes // P)
    LAST = nodes - (TILES - 1) * P
    CT = 7
    CHUNKS = TILES // CT
    assert TILES == CHUNKS * CT
    HALVES = [(0, 4), (4, CT)]
    HT = 4 * P
    COUNTED = HALF * BATCH
    GN = 10
    CW = TILES * GN
    BODY = 8
    PRE = HALF % BODY
    BODIES = HALF // BODY
    GPS = 4
    SB_STEPS = 4
    SB_GROUPS = GPS * SB_STEPS
    SBN = SB_GROUPS * GN
    GROUPS = BODIES * BODY * GPS
    SBS = GROUPS // SB_GROUPS
    SHIFT = 32
    UROWS = COUNTED // SHIFT
    UC = -(-UROWS // P)
    ULAST = UROWS - (UC - 1) * P
    GH = GROUPS // 2
    BIG = 1.0e6
    assert BODY == 2 * SB_STEPS and CW <= 512 and 2 * SBN <= 512 and PRE == 3
    WIDE = 448
    NWIDE = -(-nodes // WIDE)
    AGG = max(NWIDE * WIDE, nodes + WIN, TILES * P)

    ctx = ExitStack()
    with ctx:
        def sb(name, shape, dt=F32):
            return ctx.enter_context(nc.sbuf_tensor(name, shape, dt))

        def pb(name):
            return ctx.enter_context(nc.psum_tensor(name, [P, 512], F32))

        def sem(name):
            return ctx.enter_context(nc.semaphore(name))

        h_dram = nc.dram_tensor("h_dram", [nodes, 2 * feats], F16, kind="Internal").ap()

        hx = sb("hx", [P, TILES, P])
        xh = sb("xh", [P, TILES * P])
        h16 = xh[:, :].bitcast(F16).rearrange("p (t a f) -> p t a f", a=2, t=TILES)
        x_again = xh[:, :].rearrange("p (t f) -> p t f", t=TILES)
        agg = sb("agg", [P, 2, AGG])
        w_sb = sb("w_sb", [P, 3, P])
        wT = sb("wT", [P, 3, P])
        b_row = sb("b_row", [1, P])
        b_parts = sb("b_parts", [1, 3, P], BF16)
        b_rest = sb("b_rest", [1, P])
        ones_bf = sb("ones_bf", [1, P], BF16)
        ones = sb("ones", [P, P])
        ones16 = sb("ones16", [P, P], F16)
        ident = sb("ident", [P, P])
        iota_i = sb("iota_i", [P, 512], I32)
        iota = sb("iota", [P, 512])
        iota16 = sb("iota16", [P, 512], F16)
        part_i = sb("part_i", [P, 1], I32)
        part = sb("part", [P, 1])
        eps = sb("eps", [P, 1])
        stats = sb("stats", [P, CT, 6])
        mv = sb("mv", [P, TILES, 2])
        std = sb("std", [P, TILES])
        rstd = sb("rstd", [P, TILES])
        shift = sb("shift", [P, TILES])
        lo = sb("lo", [P, 2])
        hi = sb("hi", [P, 2])
        wide_span = sb("wide_span", [P, 2])
        diag = sb("diag", [P, 2, P])
        base = sb("base", [P, NB])
        base_i = sb("base_i", [1, NB], I32)
        flag_w = sb("flag_w", [1, 1])
        flag_c = sb("flag_c", [1, 1])
        flag_i = sb("flag_i", [1, 1], I32)
        idx = sb("idx", [P, K, NB], I32)
        rel = sb("rel", [P, K, NB])
        tail_i = sb("tail_i", [P, 2], I32)
        tail_rel = sb("tail_rel", [P, 1])
        idx_now = sb("idx_now", [P, NG_, K], I32)
        onehot = sb("onehot", [P, 2, 2, K, WIN])
        onehot16 = sb("onehot16", [P, 2, 2, K, WIN], F16)
        gathered = sb("gathered", [P, NG_, K, 2, P], F16)
        h_rest = gathered[:, :, :, :, :].rearrange("p s k a f -> p (s k a f)")[:, 0:4 * CT * P].bitcast(F32).rearrange(
            "p (s n) -> p s n", s=2)
        edge_rows = sb("edge_rows", [P, 2, 2, K, P])
        first_gt = sb("first_gt", [P, 2, GROUPS], F16)
        row0 = sb("row0", [P, UC])
        beyond = sb("beyond", [P, P])
        part32 = sb("part32", [P, 1])
        start = sb("start", [P, 2, GROUPS])
        select = sb("select", [P, NSEL, 2, GH], F16)
        key = sb("key", [P, 2, GROUPS])
        lane = sb("lane", [P, 2, GROUPS])
        first = sb("first", [P, GROUPS])
        t_a = sb("t_a", [P, 2, GH])
        t_b = sb("t_b", [P, 2, GH])
        seen = sb("seen", [P, 2])
        left = sb("left", [P, K])
        hot_key = sb("hot_key", [P, GPS, 2, CW], F16)
        hT = hot_key[:, :, :, :].rearrange("p r j c -> p (r j c)")[:, 0:4 * HT].bitcast(F32).rearrange(
            "p (s n) -> p s n", s=2)
        hot_lane = sb("hot_lane", [P, GPS, 2, P], F16)
        COUNTS = TILES * SBN
        region = sb("region", [P, max(2 * COUNTS, 2 * K * WIDE, 10 * UC * P)], F16)
        counts = [region[:, s * COUNTS:(s + 1) * COUNTS].rearrange("p (a n) -> p a n", a=TILES) for s in range(2)]
        wide_hot = region[:, 0:2 * K * WIDE].bitcast(F32).rearrange("p (k n) -> p k n", k=K)
        uv_i = region[:, 0:4 * UC * P].bitcast(I32).rearrange("p (v c e) -> p v c e", v=2, c=UC)
        half_i = region[:, 4 * UC * P:6 * UC * P].bitcast(I32).rearrange("p (c e) -> p c e", c=UC)
        rows = region[:, 6 * UC * P:6 * UC * P + 8 * BATCH].bitcast(F32).rearrange("p (a e) -> p a e", a=4)
        rows_i = rows.bitcast(I32)
        parts = region[:, 6 * UC * P:10 * UC * P].rearrange("p (v c e) -> p v c e", v=4, c=UC)

        whole = edge_rows[:, 1, 0, :, :]

        banks = [pb(f"bank{n}") for n in range(8)]
        acc = banks[0:2]
        cnt = banks[2:4]
        sums = banks[4:6]
        half = banks[6:8]
        spread = (cnt, sums)
        chosen = banks[4:8]

        s_x = [sem(f"x_loaded{c}") for c in range(CHUNKS)]
        s_w = sem("weights_loaded")
        s_rows = sem("rows_loaded")
        s_uv = sem("shifted_rows_loaded")
        s_tail_i = sem("tail_indices_loaded")
        s_const = sem("consts_ready")
        s_zero = sem("zeroed")
        s_iota = sem("iota_ready")
        s_xpad = sem("x_pad_zeroed")
        s_rowsf = sem("rows_as_float")
        s_idxc = sem("idx_copied")
        s_bparts = sem("b_parts_ready")
        s_half_i = sem("int_part_ready")
        s_parts = sem("edge_parts_ready")
        s_hot16 = sem("onehot16_ready")
        s_dve = sem("dve_step")
        s_var = sem("variance_ready")
        s_std = sem("std_ready")
        s_norm = sem("norm_ready")
        s_h = sem("h_ready")
        s_hi = sem("h_hi_ready")
        s_rest = sem("h_rest_ready")
        s_lo = sem("h_lo_ready")
        s_hstored = sem("h_stored")
        s_diag = sem("diag_ready")
        s_base = sem("base_ready")
        s_tr = sem("transposed")
        s_trc = sem("transposed_copied")
        s_wTp = sem("wT_transposed")
        s_wT = sem("wT_ready")
        s_ffill = sem("shifted_rows_filled")
        s_gt = sem("first_gt_ready")
        s_gtu = sem("first_gt_used")
        s_start = sem("starts_counted")
        s_sel = sem("select_ready")
        s_selu = sem("select_used")
        s_keyread = sem("selected_read")
        s_seen = sem("seen_ready")
        s_total = sem("seen_summed")
        s_keys = sem("keys_ready")
        s_hT = sem("hT_half_transposed")
        s_hTc = sem("hT_half_copied")
        s_u = sem("node_part_ready")
        s_uc = sem("node_part_copied")
        s_go = sem("gathers_may_go")
        s_idx = sem("idx_staged")
        s_gath = [sem(f"gathered{s}") for s in range(NG_)]
        s_gtail = sem("tail_gathered")
        s_edge = [sem(f"edges_loaded{s}") for s in range(2)]
        s_eused = sem("edges_used")
        s_step = sem("step_summed")
        s_hot = sem("onehot_ready")
        s_add = sem("added")
        s_hotp = sem("group_onehots_ready")
        s_cnt = sem("group_counted")
        s_cntc = sem("counts_copied")
        s_sums = sem("superblock_summed")
        s_flag = sem("flag_ready")
        s_gidx = sem("general_idx_staged")
        s_gg = sem("general_gathered")
        s_ge = sem("general_edges")
        s_gl = sem("general_targets")
        s_g32 = sem("general_rows_whole")
        s_gh = sem("general_onehot")
        s_gm = sem("general_summed")
        s_ga = sem("general_added")
        s_fp = sem("final_product")
        s_ft = sem("final_sum")
        s_xagain = [sem(f"x_loaded_again{c}") for c in range(CHUNKS)]
        s_fo = [sem(f"final_done{a}") for a in range(2)]
        s_out = sem("out_stored")

        def node_tiles(a, t0, t1):
            return a[t0 * P:t1 * P, :].rearrange("(t p) f -> p t f", p=P)

        def full_tiles(c):
            return CT if c < CHUNKS - 1 else CT - 1

        edge_pair = edge_attr[0:FULL * BATCH, :].rearrange("(g n p k) f -> p g n (k f)", g=2, p=P, k=K)
        edge_full = edge_attr[0:FULL * BATCH, :].rearrange("(n p k) f -> p n (k f)", p=P, k=K)
        edge_tail = edge_attr[FULL * BATCH:edges, :]

        def step_of(m, st):
            return m * BODY + (PRE + st)

        def adds_before(m):
            return 2 * (PRE - 1) if isinstance(m, int) and m == 0 else m * (2 * BODY + 4) + (2 * (PRE - 1) - 4)

        def adds_after(m, st):
            blocks = 0 if (isinstance(m, int) and m == 0) or st < 0 else 2 * (1 + (st >= SB_STEPS))
            return adds_before(m) + (2 * (st + 1) + blocks)

        ADDS = adds_before(BODIES) + 2 + 1 + 4

        block = ctx.enter_context(nc.Block())

        @block.sync
        def _(sp):
            for a, v in ((0, src), (2, dst)):
                sp.dma_start(rows_i[:, a, :], v[0:P * BATCH].rearrange("(n e) -> n e", e=BATCH)).then_inc(s_rows, 16)
                sp.dma_start(rows_i[0:ROWS2 - 1, a + 1, :],
                             v[P * BATCH:FULL * BATCH].rearrange("(n e) -> n e", e=BATCH)).then_inc(s_rows, 16)
                sp.dma_start(rows_i[ROWS2 - 1:ROWS2, a + 1, 0:TAIL],
                             v[FULL * BATCH:edges].rearrange("(n e) -> n e", n=1)).then_inc(s_rows, 16)
                sp.dma_start(rows_i[ROWS2 - 1:ROWS2, a + 1, TAIL:BATCH],
                             v[(FULL - 1) * BATCH + TAIL:FULL * BATCH].rearrange("(n e) -> n e", n=1)).then_inc(s_rows, 16)
            sp.wait_ge(s_ffill, 1)
            for a, v in ((1, dst), (0, src)):
                sp.dma_start(uv_i[:, a, 0:UC - 1, :],
                             bass.AP(v.tensor, v.offset, [[SHIFT, P], [SHIFT * P, UC - 1], [1, P]])).then_inc(s_uv, 16)
                sp.dma_start(uv_i[0:ULAST, a, UC - 1, :],
                             bass.AP(v.tensor, v.offset + SHIFT * P * (UC - 1), [[SHIFT, ULAST], [1, P]])).then_inc(s_uv, 16)
            for a, v in ((0, src), (1, dst)):
                sp.dma_start(tail_i[0:TAIL, a:a + 1], v[FULL * BATCH:edges].rearrange("(e o) -> e o", o=1)).then_inc(s_tail_i, 16)

            def load_edges(i, slot):
                sp.dma_start(edge_rows[:, slot, :, :, :].rearrange("p g k f -> p g (k f)"),
                             edge_pair[:, :, bass.ds(i, 1), :].rearrange("p g o e -> p g (o e)")).then_inc(s_edge[slot], 16)

            for i in range(2):
                load_edges(i, i % 2)
            for c in range(CHUNKS):
                sp.wait_ge(s_lo, c + 1)
                t0, t1 = c * CT, c * CT + full_tiles(c)
                sp.dma_start(node_tiles(h_dram, t0, t1),
                             h16[:, t0:t1, :, :].rearrange("p t a f -> p t (a f)")).then_inc(s_hstored, 16)
            sp.dma_start(h_dram[(TILES - 1) * P:nodes, :],
                         h16[0:LAST, TILES - 1, :, :].rearrange("p a f -> p (a f)")).then_inc(s_hstored, 16)
            for i in range(2, PRE):
                sp.wait_ge(s_eused, i - 1)
                load_edges(i, i % 2)
            with sp.Fori(0, BODIES) as m:
                for st in range(BODY):
                    i = step_of(m, st)
                    sp.wait_ge(s_eused, i - 1)
                    load_edges(i, (PRE + st) % 2)
            sp.wait_ge(s_eused, HALF - 1)
            sp.dma_start(edge_rows[0:TAIL, HALF % 2, 0, 0, :], edge_tail).then_inc(s_edge[HALF % 2], 16)

            sp.wait_ge(s_flag, 1)
            flag = sp.value_load(flag_i[0:1, 0:1], min_val=0, max_val=1)
            with sp.If(flag != 0):
                with sp.Fori(0, FULL) as n:
                    sp.wait_ge(s_ga, n * NWIDE + 1)
                    sp.dma_start(edge_rows[:, 0, 0, :, :].rearrange("p k f -> p (k f)"),
                                 edge_full[:, bass.ds(n, 1), :].rearrange("p o e -> p (o e)")).then_inc(s_ge, 16)
                sp.wait_ge(s_ga, FULL * NWIDE + 1)
                sp.dma_start(edge_rows[0:TAIL, 0, 0, 0, :], edge_tail).then_inc(s_ge, 16)

            for c in range(CHUNKS):
                for a in range(2):
                    sp.wait_ge(s_fo[a], c + 1)
                t0, t1 = c * CT, c * CT + full_tiles(c)
                sp.dma_start(node_tiles(out, t0, t1), hx[:, t0:t1, :]).then_inc(s_out, 16)
            sp.dma_start(out[(TILES - 1) * P:nodes, :], hx[0:LAST, TILES - 1, :]).then_inc(s_out, 16)
            sp.wait_ge(s_out, 16 * (CHUNKS + 1))

        @block.gpsimd
        def _(pool):
            pool.memset(ident[:, :], 0.0).then_inc(s_zero, 1)
            pool.memset(ones[:, :], 1.0).then_inc(s_const, 1)
            pool.wait_ge(s_zero, 1)
            pool.affine_select(out=ident[:, :], in_=ident[:, :], compare_op=ALU.not_equal, fill=1.0, base=0,
                               pattern=[[-1, P]], channel_multiplier=1).then_inc(s_const, 1)
            pool.iota(iota_i[:, :], pattern=[[1, 512]], base=0, channel_multiplier=0).then_inc(s_iota, 1)
            pool.iota(part_i[:, :], pattern=[[0, 1]], base=0, channel_multiplier=1).then_inc(s_iota, 1)
            pool.memset(ones16[:, :], 1.0).then_inc(s_const, 1)
            pool.memset(ones_bf[:, :], 1.0).then_inc(s_const, 1)
            pool.memset(agg[:, :, :], 0.0).then_inc(s_const, 1)

            def gather(rows_, dest, index, done):
                pool.indirect_dma_start(out=dest, out_offset=None, in_=h_dram,
                                        in_offset=bass.IndirectOffsetOnAxis(ap=index, axis=0)).then_inc(done, 16)

            def gather_batch(slot, done):
                for k in range(K):
                    gather(P, gathered[:, slot, k, :, :].rearrange("p a f -> p (a f)"), idx_now[:, slot, k:k + 1], done)

            pool.wait_ge(s_hstored, 16 * (CHUNKS + 1))
            for i in range(PRE):
                pool.wait_ge(s_idx, i + 1)
                gather_batch(i % NG_, s_gath[i % NG_])
            with pool.Fori(0, BODIES) as m:
                for st in range(BODY):
                    pool.wait_ge(s_idx, step_of(m, st) + 1)
                    pool.sem_inc(s_go, 1)
                    gather_batch((PRE + st) % NG_, s_gath[(PRE + st) % NG_])
            pool.wait_ge(s_tail_i, 32)
            pool.wait_ge(s_step, HALF - NG_ + 1)
            gather(TAIL, gathered[0:TAIL, HALF % NG_, 0, :, :].rearrange("p a f -> p (a f)"), tail_i[0:TAIL, 0:1], s_gtail)

            pool.wait_ge(s_flag, 1)
            flag = pool.value_load(flag_i[0:1, 0:1], min_val=0, max_val=1)
            with pool.If(flag != 0):
                with pool.Fori(0, FULL) as n:
                    pool.wait_ge(s_gidx, n + 1)
                    pool.sem_inc(s_go, 1)
                    gather_batch(0, s_gg)
                pool.wait_ge(s_ga, FULL * NWIDE + 1)
                gather(TAIL, gathered[0:TAIL, 0, 0, :, :].rearrange("p a f -> p (a f)"), tail_i[0:TAIL, 0:1], s_gg)

        @block.scalar
        def _(act):
            for c in range(CHUNKS):
                t0, t1 = c * CT, c * CT + full_tiles(c)
                if c == CHUNKS - 1:
                    act.wait_ge(s_xpad, 1)
                    act.dma_start(hx[0:LAST, TILES - 1, :], x[(TILES - 1) * P:nodes, :]).then_inc(s_x[c], 16)
                act.dma_start(hx[:, t0:t1, :], node_tiles(x, t0, t1)).then_inc(s_x[c], 16)
            act.dma_start(w_sb[:, :, :].rearrange("o c f -> o (c f)"), w).then_inc(s_w, 16)
            act.dma_start(b_row[0:1, :], b.rearrange("(o f) -> o f", o=1)).then_inc(s_w, 16)

            act.wait_ge(s_rows, 16 * 8)
            for a in range(4):
                n = (P, ROWS2)[a % 2]
                nc.scalar.copy(rows[0:n, a, :], rows_i[0:n, a, :]).then_inc(s_rowsf, 1)

            def deviation(c):
                t = slice(c * CT, (c + 1) * CT)
                act.wait_ge(s_var, c + 1)
                nc.scalar.activation(std[:, t], mv[:, t, 1], ACT.Sqrt, bias=eps[:, :]).then_inc(s_std, 1)

            def h_of(c):
                act.wait_ge(s_norm, c + 1)
                for t in range(c * CT, (c + 1) * CT):
                    last = nc.scalar.activation(hx[:, t, :], hx[:, t, :], ACT.Relu, bias=shift[:, t:t + 1],
                                                scale=rstd[:, t:t + 1])
                last.then_inc(s_h, 1)
                act.wait_ge(s_h, c + 1)
                nc.scalar.copy(h16[:, c * CT:(c + 1) * CT, 0, :], hx[:, c * CT:(c + 1) * CT, :]).then_inc(s_hi, 1)

            def low_part(c):
                act.wait_ge(s_rest, c + 1)
                nc.scalar.activation(h16[:, c * CT:(c + 1) * CT, 1, :],
                                     h_rest[:, c % 2, :].rearrange("p (t f) -> p t f", t=CT),
                                     ACT.Copy, scale=LO_SCALE).then_inc(s_lo, 1)

            deviation(0)
            for c in range(CHUNKS):
                if c + 1 < CHUNKS:
                    deviation(c + 1)
                h_of(c)
                if c == 0:
                    act.wait_ge(s_tr, 1)
                    for bank, (k0, k1) in zip(spread, ((0, 3), (3, K))):
                        nc.scalar.copy(idx[:, k0:k1, :], bank[0][:, 0:(k1 - k0) * NB].rearrange("p (k n) -> p k n", n=NB)
                                       ).then_inc(s_idxc, 1)
                else:
                    low_part(c - 1)
            low_part(CHUNKS - 1)

            def stage(i, slot):
                nc.scalar.copy(idx_now[:, slot, :],
                               idx[:, :, bass.ds(i + HALF, 1)].rearrange("p k o -> p (k o)")).then_inc(s_idx, 1)

            def half_onehots(i, slot):
                act.wait_ge(s_hot, i + 1)
                nc.scalar.copy(onehot16[:, slot, 0, :, :], onehot[:, slot, 1, :, :])
                nc.scalar.activation(onehot16[:, slot, 1, :, :], onehot[:, slot, 1, :, :], ACT.Copy,
                                     scale=1.0 / LO_SCALE).then_inc(s_hot16, 1)

            act.wait_ge(s_idxc, 2)
            for i in range(PRE + 1):
                stage(i, i % NG_)
            act.wait_ge(s_wTp, 1)
            nc.scalar.copy(wT[:, :, :].rearrange("f c o -> f (c o)"), half[1][:, 0:3 * P]).then_inc(s_wT, 1)
            for c in range(CHUNKS):
                for a, (t0, t1) in enumerate(HALVES):
                    n = (t1 - t0) * P
                    act.wait_ge(s_hT, 2 * c + a + 1)
                    nc.scalar.copy(hT[:, a, 0:n], half[a][:, 0:n]).then_inc(s_hTc, 1)
                for a, (t0, t1) in enumerate(HALVES):
                    n = (t1 - t0) * P
                    act.wait_ge(s_u, 2 * c + a + 1)
                    act.wait_ge(s_rest, c + 1)
                    nc.scalar.copy(hx[:, c * CT + t0:c * CT + t1, :].rearrange("p t f -> p (t f)"),
                                   half[a][:, 0:n]).then_inc(s_uc, 1)
            for v in range(4):
                act.wait_ge(s_half_i, v + 1)
                nc.scalar.copy(parts[:, v, :, :], half_i).then_inc(s_parts, 1)
            for i in range(PRE):
                half_onehots(i, i % 2)

            def act_step(m, st):
                i, slot = step_of(m, st), st // SB_STEPS
                first_body = isinstance(m, int) and m == 0
                act.wait_ge(s_step, i + 2 - NG_)
                stage(i + 1, (PRE + st + 1) % NG_)
                if st % SB_STEPS == 0 and not first_body:
                    act.wait_ge(s_sums, 2 * m + slot - 1)
                for r in range(GPS):
                    n = GPS * (st % SB_STEPS) + r
                    act.wait_ge(s_cnt, m * (BODY * GPS) + (GPS * st + r + 1))
                    nc.scalar.copy(counts[slot][:, :, n * GN:(n + 1) * GN],
                                   cnt[r % 2][:, 0:CW].rearrange("p (a d) -> p a d", d=GN)).then_inc(s_cntc, 1)
                half_onehots(i, (PRE + st) % 2)

            for st in range(BODY):
                act_step(0, st)
            with act.Fori(1, BODIES) as m:
                for st in range(BODY):
                    act_step(m, st)

            act.wait_ge(s_sums, SBS)
            for c in range(CHUNKS):
                t0, t1 = c * CT, c * CT + full_tiles(c)
                act.dma_start(x_again[:, t0:t1, :], node_tiles(x, t0, t1)).then_inc(s_xagain[c], 16)
            act.dma_start(x_again[0:LAST, TILES - 1, :], x[(TILES - 1) * P:nodes, :]).then_inc(s_xagain[CHUNKS - 1], 16)

            act.wait_ge(s_flag, 1)
            flag = act.value_load(flag_i[0:1, 0:1], min_val=0, max_val=1)
            with act.If(flag != 0):
                with act.Fori(0, FULL) as n:
                    act.wait_ge(s_ga, n * NWIDE + 1)
                    nc.scalar.copy(idx_now[:, 0, :], idx[:, :, bass.ds(n, 1)].rearrange("p k o -> p (k o)")).then_inc(s_gidx, 1)

        @block.vector
        def _(dve):
            steps = [0]

            def then(ins):
                steps[0] += 1
                ins.then_inc(s_dve, 1)
                dve.wait_ge(s_dve, steps[0])

            nc.vector.memset(hx[:, TILES - 1, :], 0.0).then_inc(s_xpad, 1)
            nc.vector.memset(uv_i[:, :, UC - 1, :], 0).then_inc(s_ffill, 1)
            then(nc.vector.memset(eps[:, :], EPS))
            for c in range(CHUNKS + 2):
                if c < CHUNKS:
                    dve.wait_ge(s_x[c], 16 if c < CHUNKS - 1 else 32)
                    for t in range(CT):
                        last = nc.vector.bn_stats(stats[:, t, :], hx[:, c * CT + t, :])
                    then(last)
                    for t in range(CT):
                        last = nc.vector.bn_aggr(mv[:, c * CT + t, :], stats[:, t, :])
                    last.then_inc(s_var, 1)
                    dve.wait_ge(s_var, c + 1)
                if 1 <= c <= CHUNKS:
                    t = slice((c - 1) * CT, c * CT)
                    dve.wait_ge(s_std, c)
                    then(nc.vector.reciprocal(rstd[:, t], std[:, t]))
                    nc.vector.scalar_tensor_tensor(out=shift[:, t], in0=mv[:, t, 0], scalar=-1.0, in1=rstd[:, t],
                                                   op0=ALU.mult, op1=ALU.mult).then_inc(s_norm, 1)
                if c >= 2:
                    n = c - 2
                    dve.wait_ge(s_hi, n + 1)
                    if n >= 2:
                        dve.wait_ge(s_lo, n - 1)
                    nc.vector.scalar_tensor_tensor(
                        out=h_rest[:, n % 2, :].rearrange("p (t f) -> p t f", t=CT),
                        in0=h16[:, n * CT:(n + 1) * CT, 0, :], scalar=-1.0, in1=hx[:, n * CT:(n + 1) * CT, :],
                        op0=ALU.mult, op1=ALU.add).then_inc(s_rest, 1)
            dve.wait_ge(s_w, 32)
            then(nc.vector.tensor_copy(b_parts[0:1, 0, :], b_row[0:1, :]))
            then(nc.vector.tensor_tensor(b_rest[0:1, :], b_row[0:1, :], b_parts[0:1, 0, :], ALU.subtract))
            then(nc.vector.tensor_copy(b_parts[0:1, 1, :], b_rest[0:1, :]))
            nc.vector.tensor_tensor(b_parts[0:1, 2, :], b_rest[0:1, :], b_parts[0:1, 1, :],
                                    ALU.subtract).then_inc(s_bparts, 1)

            dve.wait_ge(s_rowsf, 4)
            nr = (P, ROWS2)
            for a in range(2):
                nc.vector.tensor_reduce(lo[0:nr[a], a:a + 1], rows[0:nr[a], 2 + a, :], AX, ALU.min)
                last = nc.vector.tensor_reduce(hi[0:nr[a], a:a + 1], rows[0:nr[a], 2 + a, :], AX, ALU.max)
            then(last)
            dve.wait_ge(s_const, 3)
            for a in range(2):
                nc.vector.tensor_scalar(diag[0:nr[a], a, 0:nr[a]], ident[0:nr[a], 0:nr[a]], lo[0:nr[a], a:a + 1], None,
                                        ALU.mult)
                last = nc.vector.tensor_tensor(hi[0:nr[a], a:a + 1], hi[0:nr[a], a:a + 1], lo[0:nr[a], a:a + 1],
                                               ALU.subtract)
            then(last)
            for a in range(2):
                last = nc.vector.tensor_scalar(wide_span[0:nr[a], a:a + 1], hi[0:nr[a], a:a + 1], float(WIN), None, ALU.is_ge)
            last.then_inc(s_diag, 1)
            dve.wait_ge(s_iota, 2)
            nc.vector.tensor_copy(iota[:, :], iota_i[:, :])
            nc.vector.tensor_copy(iota16[:, :], iota_i[:, :])
            then(nc.vector.tensor_copy(part[:, :], part_i[:, :]))
            dve.wait_ge(s_base, 1)
            nc.vector.tensor_copy(base[:, :], half[0][:, 0:NB])
            nc.vector.tensor_copy(base_i[0:1, :], half[0][0:1, 0:NB])
            then(nc.vector.tensor_copy(flag_w[0:1, 0:1], half[0][0:1, NB:NB + 1]))
            dve.wait_ge(s_tr, 2)
            for bank, (k0, k1) in zip(spread, ((0, 3), (3, K))):
                nc.vector.tensor_tensor(rel[:, k0:k1, :], bank[1][:, 0:(k1 - k0) * NB].rearrange("p (k n) -> p k n", n=NB),
                                        base[:, :].unsqueeze(1).broadcast_to([P, k1 - k0, NB]),
                                        ALU.subtract).then_inc(s_trc, 1)
            dve.wait_ge(s_trc, 2)
            dve.wait_ge(s_tail_i, 32)
            nc.vector.tensor_tensor(tail_rel[0:TAIL, :], tail_i[0:TAIL, 1:2], base[0:TAIL, FULL:NB], ALU.subtract)

            def make_onehot(i, slot):
                for g in range(2):
                    last = nc.vector.tensor_tensor(onehot[:, slot, g, :, :],
                                                   rel[:, :, bass.ds(i + g * HALF, 1)].broadcast_to([P, K, WIN]),
                                                   iota[:, 0:WIN].unsqueeze(1).broadcast_to([P, K, WIN]), ALU.is_equal)
                last.then_inc(s_hot, 1)

            for i in range(2):
                make_onehot(i, i)

            dve.wait_ge(s_uv, 64)
            nc.vector.tensor_copy(row0[:, :], uv_i[:, 1, :, 0])
            nc.vector.tensor_scalar(first[:, :], iota[:, 0:GROUPS], float(GN), None, ALU.mult)
            then(nc.vector.tensor_scalar(part32[:, :], part[:, :], float(SHIFT), None, ALU.mult))
            then(nc.vector.tensor_scalar(beyond[:, :], iota[:, 0:P], part32[:, 0:1],
                                         float(COUNTED - SHIFT * P * (UC - 1)), ALU.add, ALU.is_ge))
            then(nc.vector.scalar_tensor_tensor(out=row0[:, UC - 1:UC], in0=beyond[:, 0:1], scalar=BIG,
                                                in1=row0[:, UC - 1:UC], op0=ALU.mult, op1=ALU.add))
            for c in range(UC):
                if c >= 2:
                    dve.wait_ge(s_gtu, c - 1)
                nc.vector.tensor_scalar(first_gt[:, c % 2, :], first[:, :], row0[:, c:c + 1], None,
                                        ALU.is_gt).then_inc(s_gt, 1)
            for v in range(2):
                for o, (n, op) in enumerate(((7, ALU.arith_shift_right), (P - 1, ALU.bitwise_and))):
                    if v or o:
                        dve.wait_ge(s_parts, 2 * v + o)
                    nc.vector.tensor_scalar(half_i, uv_i[:, v, :, :], n, None, op).then_inc(s_half_i, 1)
            dve.wait_ge(s_start, 1)
            t_start = t_a[:, :, :].rearrange("p j g -> p (j g)")
            then(nc.vector.tensor_scalar(t_start, sums[0][:, 0:GROUPS], -1.0, 0.0, ALU.add, ALU.max))
            for j in range(2):
                last = nc.vector.tensor_scalar(start[:, j, :], t_start, part[:, 0:1], float(j * P // SHIFT),
                                               ALU.subtract, ALU.add)
            then(last)
            dve.wait_ge(s_parts, 4)
            then(nc.vector.scalar_tensor_tensor(out=parts[:, 2, UC - 1, :], in0=beyond[:, :], scalar=float(P),
                                                in1=parts[:, 2, UC - 1, :], op0=ALU.mult, op1=ALU.add))
            for hh in range(2):
                g = slice(hh * GH, (hh + 1) * GH)
                for c in range(UC):
                    n = hh * UC + c
                    if n >= NSEL:
                        dve.wait_ge(s_selu, n + 1 - NSEL)
                    nc.vector.tensor_scalar(select[:, n % NSEL, :, :], start[:, :, g], float(c * P), None,
                                            ALU.is_equal).then_inc(s_sel, 1)
                dve.wait_ge(s_selu, (hh + 1) * UC)
                tile_, lane_, dhi, dlo = (z[:, 0:2 * GH].rearrange("p (j g) -> p j g", j=2) for z in chosen)
                nc.vector.tensor_copy(lane[:, :, g], lane_)
                nc.vector.tensor_copy(t_b[:, :, :], dlo)
                then(nc.vector.tensor_copy(key[:, :, g], tile_))
                nc.vector.scalar_tensor_tensor(out=t_a[:, :, :], in0=dhi, scalar=float(P), in1=t_b[:, :, :],
                                               op0=ALU.mult, op1=ALU.add).then_inc(s_keyread, 1)
                dve.wait_ge(s_keyread, hh + 1)
                then(nc.vector.tensor_tensor(t_a[:, :, :], t_a[:, :, :],
                                             first[:, g].unsqueeze(1).broadcast_to([P, 2, GH]), ALU.subtract))
                then(nc.vector.tensor_scalar(t_b[:, :, :], t_a[:, :, :], 0.0, None, ALU.is_ge))
                then(nc.vector.scalar_tensor_tensor(out=t_b[:, :, :], in0=t_a[:, :, :], scalar=float(GN - 1),
                                                    in1=t_b[:, :, :], op0=ALU.is_le, op1=ALU.mult))
                then(nc.vector.tensor_reduce(seen[:, hh:hh + 1], t_b[:, :, :].rearrange("p j g -> p (j g)"), AX, ALU.add))
                then(nc.vector.scalar_tensor_tensor(out=t_a[:, :, :], in0=key[:, :, g], scalar=float(GN),
                                                    in1=t_a[:, :, :], op0=ALU.mult, op1=ALU.add))
                then(nc.vector.scalar_tensor_tensor(out=t_a[:, :, :], in0=t_a[:, :, :], scalar=1.0,
                                                    in1=t_b[:, :, :], op0=ALU.add, op1=ALU.mult))
                nc.vector.tensor_scalar(key[:, :, g], t_a[:, :, :], -1.0, None, ALU.add).then_inc(s_keys, 1)
            dve.wait_ge(s_keys, 2)
            dve.wait_ge(s_total, 1)
            then(nc.vector.tensor_copy(flag_c[0:1, 0:1], half[0][0:1, 0:1]))
            then(nc.vector.tensor_scalar(flag_c[0:1, 0:1], half[0][0:1, 1:2], flag_c[0:1, 0:1], float(COUNTED),
                                         ALU.add, ALU.not_equal))
            then(nc.vector.tensor_tensor(flag_c[0:1, 0:1], flag_c[0:1, 0:1], flag_w[0:1, 0:1], ALU.add))
            nc.vector.tensor_scalar(flag_i[0:1, 0:1], flag_c[0:1, 0:1], 1.0, None, ALU.min).then_inc(s_flag, 1)
            def add_window(n, slot, col, before):
                at = dve.value_load(base_i[0:1, bass.ds(n, 1)], min_val=0, max_val=nodes - 1)
                dve.wait_ge(s_add, before)
                a = 2 if col else 1
                nc.vector.tensor_tensor(agg[:, 0:a, bass.ds(at, WIN)], agg[:, 0:a, bass.ds(at, WIN)],
                                        acc[slot][:, col:col + a * WIN].rearrange("p (a w) -> p a w", a=a),
                                        ALU.add).then_inc(s_add, 1)

            def add_step(i, slot, before):
                dve.wait_ge(s_step, i + 1)
                add_window(i, slot, 0, before)
                add_window(i + HALF, slot, WIN, before + 1)

            def add_superblock(n, slot, before):
                dve.wait_ge(s_sums, n + 1)
                dve.wait_ge(s_add, before)
                at = agg[:, 1, bass.ds(n * SBN, SBN)]
                nc.vector.scalar_tensor_tensor(out=at, in0=sums[slot][:, SBN:2 * SBN], scalar=1.0 / LO_SCALE, in1=at,
                                               op0=ALU.mult, op1=ALU.add).then_inc(s_add, 1)
                dve.wait_ge(s_add, before + 1)
                nc.vector.tensor_tensor(at, at, sums[slot][:, 0:SBN], ALU.add).then_inc(s_add, 1)

            dve.wait_ge(s_const, 5)
            add_step(0, 0, 0)
            make_onehot(2, 0)
            add_step(1, 1, 2)

            def dve_step(m, st):
                i = step_of(m, st)
                first_body = isinstance(m, int) and m == 0
                before = adds_after(m, st - 1)
                if st % SB_STEPS == 0 and not first_body:
                    slot = st // SB_STEPS
                    add_superblock(2 * m + (slot - 2), slot, before)
                    before = before + 2
                for r in range(GPS):
                    g = m * (BODY * GPS) + (GPS * st + r)
                    if not (first_body and st == 0):
                        dve.wait_ge(s_cnt, g + (1 - GPS))
                    for j in range(2):
                        nc.vector.tensor_scalar(hot_key[:, r, j, :], iota16[:, 0:CW], key[:, j, bass.ds(g, 1)], None,
                                                ALU.is_equal)
                        last = nc.vector.tensor_scalar(hot_lane[:, r, j, :], iota16[:, 0:P], lane[:, j, bass.ds(g, 1)],
                                                       None, ALU.is_equal)
                    last.then_inc(s_hotp, 1)
                dve.wait_ge(s_step, i - 1)
                make_onehot(i, (PRE + st) % 2)
                add_step(i - 1, (PRE + st - 1) % 2, before)

            for st in range(BODY):
                dve_step(0, st)
            with dve.Fori(1, BODIES) as m:
                for st in range(BODY):
                    dve_step(m, st)
            done = adds_before(BODIES)
            slot = HALF % 2
            dve.wait_ge(s_step, HALF - 1)
            nc.vector.tensor_tensor(onehot[0:TAIL, slot, 0, 0, :], tail_rel[0:TAIL, 0:1].broadcast_to([TAIL, WIN]),
                                    iota[0:TAIL, 0:WIN], ALU.is_equal).then_inc(s_hot, 1)
            dve.wait_ge(s_hot, HALF + 1)
            nc.vector.tensor_copy(onehot16[0:TAIL, slot, 0, 0, :], onehot[0:TAIL, slot, 0, 0, :])
            nc.vector.tensor_scalar(onehot16[0:TAIL, slot, 1, 0, :], onehot[0:TAIL, slot, 0, 0, :], 1.0 / LO_SCALE,
                                    None, ALU.mult).then_inc(s_hot, 1)
            add_step(HALF - 1, (HALF - 1) % 2, done)
            add_superblock(SBS - 2, SBS % 2, done + 2)
            dve.wait_ge(s_step, HALF + 1)
            add_window(FULL, slot, WIN, done + 4)
            add_superblock(SBS - 1, (SBS - 1) % 2, done + 5)

            dve.wait_ge(s_add, ADDS)
            dve.wait_ge(s_flag, 1)
            flag = dve.value_load(flag_i[0:1, 0:1], min_val=0, max_val=1)
            with dve.If(flag != 0):
                nc.vector.memset(agg[:, :, :], 0.0).then_inc(s_ga, 1)

                def wide_sums(ks, windows, targets):
                    with dve.Fori(0, NWIDE) as j:
                        dve.wait_ge(s_gl, targets)
                        nc.vector.tensor_tensor(wide_hot[:, 0:ks, :],
                                                left[:, 0:ks].unsqueeze(2).broadcast_to([P, ks, WIDE]),
                                                iota[:, 0:WIDE].unsqueeze(1).broadcast_to([P, ks, WIDE]),
                                                ALU.is_equal).then_inc(s_gh, 1)
                        dve.wait_ge(s_gh, windows + j + 1)
                        nc.vector.tensor_scalar(left[:, :], left[:, :], -float(WIDE), None, ALU.add)
                        dve.wait_ge(s_gm, windows + j + 1)
                        for a in range(2):
                            at = agg[:, a, bass.ds(j * WIDE, WIDE)]
                            last = nc.vector.tensor_tensor(at, at, cnt[a][:, 0:WIDE], ALU.add)
                        last.then_inc(s_ga, 1)
                        dve.wait_ge(s_ga, windows + j + 2)

                with dve.Fori(0, FULL) as n:
                    dve.wait_ge(s_ga, n * NWIDE + 1)
                    nc.vector.tensor_scalar(left[:, :], rel[:, :, bass.ds(n, 1)].rearrange("p k o -> p (k o)"),
                                            base[:, bass.ds(n, 1)], None, ALU.add).then_inc(s_gl, 1)
                    dve.wait_ge(s_gg, (16 * K) * n + 16 * K)
                    nc.vector.scalar_tensor_tensor(out=whole, in0=gathered[:, 0, :, 1, :], scalar=1.0 / LO_SCALE,
                                                   in1=gathered[:, 0, :, 0, :], op0=ALU.mult,
                                                   op1=ALU.add).then_inc(s_g32, 1)
                    wide_sums(K, n * NWIDE, n + 1)
                nc.vector.tensor_copy(left[0:TAIL, 0:1], tail_i[0:TAIL, 1:2]).then_inc(s_gl, 1)
                dve.wait_ge(s_gg, 16 * K * FULL + 16)
                nc.vector.scalar_tensor_tensor(out=whole[0:TAIL, 0, :], in0=gathered[0:TAIL, 0, 0, 1, :],
                                               scalar=1.0 / LO_SCALE, in1=gathered[0:TAIL, 0, 0, 0, :], op0=ALU.mult,
                                               op1=ALU.add).then_inc(s_g32, 1)
                wide_sums(1, FULL * NWIDE, FULL + 1)

            for c in range(CHUNKS):
                dve.wait_ge(s_xagain[c], 16 if c < CHUNKS - 1 else 32)
                for a, (t0, t1) in enumerate(HALVES):
                    n = (t1 - t0) * P
                    o = hx[:, CT * c + t0:CT * c + t1, :].rearrange("p t f -> p (t f)")
                    xs = x_again[:, CT * c + t0:CT * c + t1, :].rearrange("p t f -> p (t f)")
                    dve.wait_ge(s_fp, 2 * c + a + 1)
                    nc.vector.tensor_tensor(o, o, half[a][:, 0:n], ALU.add).then_inc(s_ft, 1)
                    dve.wait_ge(s_ft, 2 * c + a + 1)
                    nc.vector.scalar_tensor_tensor(out=o, in0=o, scalar=0.0, in1=xs, op0=ALU.max,
                                                   op1=ALU.add).then_inc(s_fo[a], 1)

        @block.tensor
        def _(pe):
            nr = (P, ROWS2)
            pe.wait_ge(s_const, 3)
            for v in range(2):
                pe.wait_ge(s_rowsf, 2 * v + 2)
                for bank, (k0, k1) in zip(spread, ((0, 3), (3, K))):
                    for k in range(k0, k1):
                        for a in range(2):
                            c0 = (k - k0) * NB + a * P
                            last = nc.tensor.transpose(
                                bank[v][:, c0:c0 + nr[a]],
                                rows[0:nr[a], 2 * v + a, :].rearrange("n (p k) -> n k p", k=K)[:, k, :],
                                ident[0:nr[a], 0:nr[a]])
                last.then_inc(s_tr, 1)
            pe.wait_ge(s_w, 32)
            for c in range(3):
                last = nc.tensor.transpose(half[1][:, c * P:(c + 1) * P], w_sb[:, c, :], ident[:, :])
            last.then_inc(s_wTp, 1)
            pe.wait_ge(s_diag, 1)
            for a in range(2):
                nc.tensor.matmul(half[0][:, a * P:a * P + nr[a]], ones[0:nr[a], :], diag[0:nr[a], a, 0:nr[a]],
                                 start=True, stop=True)
            nc.tensor.matmul(half[0][:, NB:NB + 1], ones[:, :], wide_span[:, 0:1], start=True, stop=False)
            nc.tensor.matmul(half[0][:, NB:NB + 1], ones[0:ROWS2, :], wide_span[0:ROWS2, 1:2], start=False,
                             stop=True).then_inc(s_base, 1)
            pe.wait_ge(s_trc, 1)
            pe.wait_ge(s_wT, 1)
            pe.wait_ge(s_bparts, 1)
            pe.wait_ge(s_const, 5)
            for c in range(CHUNKS):
                pe.wait_ge(s_h, c + 1)
                for a, (t0, t1) in enumerate(HALVES):
                    if c:
                        pe.wait_ge(s_uc, 2 * c + a - 1)
                    for t in range(t0, t1):
                        last = nc.tensor.transpose(half[a][:, (t - t0) * P:(t - t0 + 1) * P], hx[:, c * CT + t, :],
                                                   ident[:, :])
                    last.then_inc(s_hT, 1)
                for a, (t0, t1) in enumerate(HALVES):
                    n = t1 - t0
                    pe.wait_ge(s_hTc, 2 * c + a + 1)
                    for v in range(3):
                        nc.tensor.matmul(half[a][:, 0:n * P], ones_bf[0:1, :],
                                         b_parts[0:1, v:v + 1, :].broadcast_to([1, n, P]),
                                         start=(v == 0), stop=False)
                    for t in range(n):
                        o = slice(t * P, (t + 1) * P)
                        last = nc.tensor.matmul(half[a][:, o], hT[:, a, o], wT[:, 0, :], start=False, stop=(t == n - 1))
                    last.then_inc(s_u, 1)

            def products(out_, rows_, left_, right):
                for k in range(len(left_)):
                    last = nc.tensor.matmul(out_, left_[k][0:rows_], right[k][0:rows_], start=(k == 0),
                                            stop=(k == len(left_) - 1))
                return last

            def by_k(v):
                return [v[:, k, :] for k in range(K)]

            pe.wait_ge(s_idxc, 2)
            pe.wait_ge(s_trc, 2)
            for c in range(UC):
                pe.wait_ge(s_gt, c + 1)
                last = nc.tensor.matmul(sums[0][:, 0:GROUPS], ones16[:, :], first_gt[:, c % 2, :], start=(c == 0),
                                        stop=(c == UC - 1))
                last.then_inc(s_gtu if c < UC - 1 else s_start, 1)
            pe.wait_ge(s_uc, 2 * CHUNKS)
            for hh in range(2):
                if hh:
                    pe.wait_ge(s_keyread, 1)
                for c in range(UC):
                    pe.wait_ge(s_sel, hh * UC + c + 1)
                    for v in range(4):
                        last = nc.tensor.matmul(chosen[v][:, 0:2 * GH], parts[:, v, c, :],
                                                select[:, (hh * UC + c) % NSEL, :, :].rearrange("p j g -> p (j g)"),
                                                start=(c == 0), stop=(c == UC - 1))
                    last.then_inc(s_selu, 1)
            pe.wait_ge(s_keys, 2)
            nc.tensor.matmul(half[0][:, 0:2], ones[:, :], seen[:, :], start=True, stop=True).then_inc(s_total, 1)

            def sum_step(i, slot, gslot, fill, gfill):
                pe.wait_ge(s_edge[slot], 16 * fill + 16)
                pe.wait_ge(s_hot, i + 1)
                for g in range(2):
                    last = products(acc[slot][:, g * WIN:(g + 1) * WIN], P, by_k(edge_rows[:, slot, g, :, :]),
                                    by_k(onehot[:, slot, g, :, :]))
                last.then_inc(s_eused, 1)
                pe.wait_ge(s_gath[gslot], (16 * K) * gfill + 16 * K)
                pe.wait_ge(s_hot16, i + 1)
                products(acc[slot][:, 2 * WIN:3 * WIN], P,
                         [gathered[:, gslot, k, a, :] for k in range(K) for a in range(2)],
                         [onehot16[:, slot, a, k, :] for k in range(K) for a in range(2)]).then_inc(s_step, 1)

            for i in range(PRE):
                if i == 2:
                    pe.wait_ge(s_add, 2)
                sum_step(i, i % 2, i % NG_, i // 2, i // NG_)
            pe.wait_ge(s_lo, CHUNKS)

            def sum_superblock(slot, part, a0, a1):
                for a in range(a0, a1):
                    last = nc.tensor.matmul(sums[slot][:, part * SBN:(part + 1) * SBN], h16[:, a, part, :],
                                            counts[slot][:, a, :], start=(a == 0), stop=(a == TILES - 1))
                return last

            QUARTERS = [(0, 0, (TILES + 1) // 2), (0, (TILES + 1) // 2, TILES),
                        (1, 0, (TILES + 1) // 2), (1, (TILES + 1) // 2, TILES)]

            def pe_step(m, st):
                i = step_of(m, st)
                first_body = isinstance(m, int) and m == 0

                def count(groups):
                    for r in groups:
                        g = m * (BODY * GPS) + (GPS * st + r)
                        pe.wait_ge(s_hotp, g + 1)
                        if not (first_body and st == 0 and r < 2):
                            pe.wait_ge(s_cntc, g - 1)
                        for j in range(2):
                            last = nc.tensor.matmul(cnt[r % 2][:, 0:CW], hot_lane[:, r, j, :], hot_key[:, r, j, :],
                                                    start=(j == 0), stop=(j == 1))
                        last.then_inc(s_cnt, 1)

                count((0, 1))
                later, quarter = divmod(st, SB_STEPS)
                if later or not first_body:
                    slot = 1 - later
                    if quarter == 0:
                        pe.wait_ge(s_cntc, m * (2 * SB_GROUPS) + SB_GROUPS * later)
                        if not first_body:
                            pe.wait_ge(s_add, adds_after(m, 0) - 2 if later else m * (2 * BODY + 4) - BODY)
                    last = sum_superblock(slot, *QUARTERS[quarter])
                    if quarter == SB_STEPS - 1:
                        last.then_inc(s_sums, 1)
                count((2, 3))
                pe.wait_ge(s_add, adds_after(m, st - 1))
                sum_step(i, (PRE + st) % 2, (PRE + st) % NG_, m * (BODY // 2) + (PRE + st) // 2,
                         m * (BODY // NG_) + (PRE + st) // NG_)

            for st in range(BODY):
                pe_step(0, st)
            with pe.Fori(1, BODIES) as m:
                for st in range(BODY):
                    pe_step(m, st)

            slot, fill = HALF % 2, HALF // 2
            pe.wait_ge(s_edge[slot], 16 * (fill + 1))
            pe.wait_ge(s_gtail, 16)
            pe.wait_ge(s_hot, HALF + 2)
            pe.wait_ge(s_add, adds_before(BODIES))
            products(acc[slot][:, WIN:2 * WIN], TAIL, [edge_rows[:, slot, 0, 0, :]], [onehot[:, slot, 0, 0, :]])
            products(acc[slot][:, 2 * WIN:3 * WIN], TAIL, [gathered[:, HALF % NG_, 0, a, :] for a in range(2)],
                     [onehot16[:, slot, a, 0, :] for a in range(2)]).then_inc(s_step, 1)
            slot = (SBS - 1) % 2
            pe.wait_ge(s_cntc, GROUPS)
            for q in QUARTERS:
                last = sum_superblock(slot, *q)
            last.then_inc(s_sums, 1)

            pe.wait_ge(s_add, ADDS)
            flag = pe.value_load(flag_i[0:1, 0:1], min_val=0, max_val=1)
            with pe.If(flag != 0):
                def wide_products(rows_, ks, done):
                    pe.wait_ge(s_gh, done + 1)
                    pe.wait_ge(s_ga, done + 1)
                    for o, v in ((cnt[0], edge_rows[:, 0, 0, :, :]), (cnt[1], whole)):
                        last = products(o[:, 0:WIDE], rows_, by_k(v)[0:ks], by_k(wide_hot)[0:ks])
                    last.then_inc(s_gm, 1)

                with pe.Fori(0, FULL) as n:
                    with pe.Fori(0, NWIDE) as j:
                        pe.wait_ge(s_ge, 16 * n + 16)
                        pe.wait_ge(s_g32, n + 1)
                        wide_products(P, K, n * NWIDE + j)
                pe.wait_ge(s_ge, 16 * NB)
                pe.wait_ge(s_g32, NB)
                with pe.Fori(0, NWIDE) as j:
                    wide_products(TAIL, 1, FULL * NWIDE + j)
                pe.wait_ge(s_ga, NB * NWIDE + 1)

            for c in range(CHUNKS):
                for a, (t0, t1) in enumerate(HALVES):
                    if c:
                        pe.wait_ge(s_fo[a], c)
                    for t in range(t0, t1):
                        o = half[a][:, (t - t0) * P:(t - t0 + 1) * P]
                        n = slice((c * CT + t) * P, (c * CT + t + 1) * P)
                        nc.tensor.matmul(o, agg[:, 1, n], wT[:, 1, :], start=True, stop=False)
                        last = nc.tensor.matmul(o, agg[:, 0, n], wT[:, 2, :], start=False, stop=True)
                    last.then_inc(s_fp, 1)


_INS = ["x", "src", "dst", "edge_attr_128", "L0_gnn_W", "L0_gnn_b"]


def kernel(**inputs):
    import concourse.bacc as bacc
    from concourse.bass_utils import run_bass_kernel_spmd

    nc = bacc.Bacc("TRN2", target_bir_lowering=False, num_devices=1)
    arrays, args = {}, []
    for name in _INS:
        a = np.ascontiguousarray(inputs[name])
        arrays[f"in_{name}"] = a
        args.append(nc.dram_tensor(f"in_{name}", a.shape, mybir.dt.from_np(a.dtype), kind="ExternalInput").ap())
    shape = inputs["x"].shape
    args.append(nc.dram_tensor("result", shape, F32, kind="ExternalOutput").ap())
    build(nc, *args)
    r = run_bass_kernel_spmd(nc, [arrays], core_ids=[0])
    return r.results[0]["result"]
```

```python
import numpy as np
import concourse.bass as bass
import concourse.mybir as mybir
from concourse.alu_op_type import AluOpType as ALU
from contextlib import ExitStack

F32 = mybir.dt.float32
F16 = mybir.dt.float16
I32 = mybir.dt.int32
ACT = mybir.ActivationFunctionType
AX = mybir.AxisListType.X
P = 128
EPS = 1e-5
LO_SCALE = 2.0 ** 11


def build(nc, x, src, dst, edge_attr, w, b, out):
    nodes, feats = x.shape
    edges = src.shape[0]
    assert feats == P
    K = 5
    BATCH = K * P
    FULL = edges // BATCH
    TAIL = edges - FULL * BATCH
    assert 2 <= TAIL <= P and FULL % 2 == 0
    HALF = FULL // 2
    NB = FULL + 1
    ROWS2 = NB - P
    WIN = 48
    NG_ = 4
    NSEL = 4
    TILES = -(-nodes // P)
    LAST = nodes - (TILES - 1) * P
    CT = 7
    CHUNKS = TILES // CT
    assert TILES == CHUNKS * CT
    HALVES = [(0, 4), (4, CT)]
    HT = 4 * P
    COUNTED = HALF * BATCH
    GN = 10
    CW = TILES * GN
    BODY = 8
    PRE = HALF % BODY
    BODIES = HALF // BODY
    GPS = 4
    SB_STEPS = 4
    SB_GROUPS = GPS * SB_STEPS
    SBN = SB_GROUPS * GN
    GROUPS = BODIES * BODY * GPS
    SBS = GROUPS // SB_GROUPS
    SHIFT = 32
    UROWS = COUNTED // SHIFT
    UC = -(-UROWS // P)
    ULAST = UROWS - (UC - 1) * P
    GH = GROUPS // 2
    BIG = 1.0e6
    assert BODY == 2 * SB_STEPS and CW <= 512 and 2 * SBN <= 512 and PRE == 3
    WIDE = 448
    NWIDE = -(-nodes // WIDE)
    AGG = max(NWIDE * WIDE, nodes + WIN, TILES * P)
    assert CHUNKS == 7

    ctx = ExitStack()
    with ctx:
        def sb(name, shape, dt=F32):
            return ctx.enter_context(nc.sbuf_tensor(name, shape, dt))

        def pb(name):
            return ctx.enter_context(nc.psum_tensor(name, [P, 512], F32))

        def sem(name):
            return ctx.enter_context(nc.semaphore(name))

        h_dram = nc.dram_tensor("h_dram", [nodes, 2 * feats], F16, kind="Internal").ap()

        hx = sb("hx", [P, TILES, P])
        xh = sb("xh", [P, TILES * P])
        h16 = xh[:, :].bitcast(F16).rearrange("p (t a f) -> p t a f", a=2, t=TILES)
        x_again = xh[:, :].rearrange("p (t f) -> p t f", t=TILES)
        agg = sb("agg", [P, 2, AGG])
        hT = sb("hT", [P, 2, HT])
        w_sb = sb("w_sb", [P, 3, P])
        wT = sb("wT", [P, 3, P])
        b_all = sb("b_all", [P, P])
        ones = sb("ones", [P, P])
        ones16 = sb("ones16", [P, P], F16)
        ident = sb("ident", [P, P])
        iota_i = sb("iota_i", [P, 512], I32)
        iota = sb("iota", [P, 512])
        iota16 = sb("iota16", [P, 512], F16)
        part_i = sb("part_i", [P, 1], I32)
        part = sb("part", [P, 1])
        eps = sb("eps", [P, 1])
        stats = sb("stats", [P, CT, 6])
        mv = sb("mv", [P, TILES, 2])
        std = sb("std", [P, TILES])
        rstd = sb("rstd", [P, TILES])
        shift = sb("shift", [P, TILES])
        lo = sb("lo", [P, 2])
        hi = sb("hi", [P, 2])
        wide_span = sb("wide_span", [P, 2])
        diag = sb("diag", [P, 2, P])
        base = sb("base", [P, NB])
        base_i = sb("base_i", [1, NB], I32)
        flag_w = sb("flag_w", [1, 1])
        flag_c = sb("flag_c", [1, 1])
        flag_i = sb("flag_i", [1, 1], I32)
        idx = sb("idx", [P, K, NB], I32)
        rel = sb("rel", [P, K, NB])
        tail_i = sb("tail_i", [P, 2], I32)
        tail_rel = sb("tail_rel", [P, 1])
        idx_now = sb("idx_now", [P, NG_, K], I32)
        onehot = sb("onehot", [P, 2, 2, K, WIN])
        onehot16 = sb("onehot16", [P, 2, 2, K, WIN], F16)
        gathered = sb("gathered", [P, NG_, K, 2, P], F16)
        h_rest = gathered[:, :, :, :, :].rearrange("p s k a f -> p (s k a f)")[:, 0:4 * CT * P].bitcast(F32).rearrange(
            "p (s n) -> p s n", s=2)
        edge_rows = sb("edge_rows", [P, 2, 2, K, P])
        row0 = sb("row0", [P, UC])
        beyond = sb("beyond", [P, P])
        part32 = sb("part32", [P, 1])
        start = sb("start", [P, 2, GROUPS])
        select = sb("select", [P, NSEL, 2, GH], F16)
        first_gt = select[:, :, :, :].rearrange("p s j g -> p s (j g)")
        key = sb("key", [P, 2, GROUPS])
        lane = sb("lane", [P, 2, GROUPS])
        first = sb("first", [P, GROUPS])
        t_a = sb("t_a", [P, 2, GH])
        t_b = sb("t_b", [P, 2, GH])
        seen = sb("seen", [P, 2])
        left = sb("left", [P, K])
        hot_key = sb("hot_key", [P, GPS, 2, CW], F16)
        hot_lane = sb("hot_lane", [P, GPS, 2, P], F16)
        COUNTS = TILES * SBN
        region = sb("region", [P, max(2 * COUNTS, 2 * K * WIDE, 10 * UC * P)], F16)
        counts = [region[:, s * COUNTS:(s + 1) * COUNTS].rearrange("p (a n) -> p a n", a=TILES) for s in range(2)]
        wide_hot = region[:, 0:2 * K * WIDE].bitcast(F32).rearrange("p (k n) -> p k n", k=K)
        uv_i = region[:, 0:4 * UC * P].bitcast(I32).rearrange("p (v c e) -> p v c e", v=2, c=UC)
        half_i = region[:, 4 * UC * P:6 * UC * P].bitcast(I32).rearrange("p (c e) -> p c e", c=UC)
        rows = region[:, 6 * UC * P:6 * UC * P + 8 * BATCH].bitcast(F32).rearrange("p (a e) -> p a e", a=4)
        rows_i = rows.bitcast(I32)
        parts = region[:, 6 * UC * P:10 * UC * P].rearrange("p (v c e) -> p v c e", v=4, c=UC)

        whole = edge_rows[:, 1, 0, :, :]

        banks = [pb(f"bank{n}") for n in range(8)]
        acc = banks[0:2]
        cnt = banks[2:4]
        sums = banks[4:6]
        half = banks[6:8]
        spread = (cnt, sums)
        chosen = banks[2:6]

        s_x = [sem(f"x_loaded{c}") for c in range(CHUNKS)]
        s_w = sem("weights_loaded")
        s_b = sem("bias_loaded")
        s_rows = [sem(f"{v}_rows_loaded") for v in ("dst", "src")]
        s_uv = sem("shifted_rows_loaded")
        s_tail_i = sem("tail_indices_loaded")
        s_const = sem("consts_ready")
        s_zero = sem("zeroed")
        s_iota = sem("iota_ready")
        s_xpad = sem("x_pad_zeroed")
        s_rowsf = [sem(f"{v}_rows_as_float") for v in ("dst", "src")]
        s_idxc = sem("idx_copied")
        s_half_i = sem("high_int_part_ready")
        s_low_i = sem("low_int_part_ready")
        s_parts = sem("high_edge_parts_ready")
        s_lparts = sem("low_edge_parts_ready")
        s_hot16 = sem("onehot16_ready")
        s_dve = sem("dve_step")
        s_var = sem("variance_ready")
        s_std = sem("std_ready")
        s_norm = sem("norm_ready")
        s_h = sem("h_ready")
        s_hi = sem("h_hi_ready")
        s_rest = sem("h_rest_ready")
        s_lo = sem("h_lo_ready")
        s_hstored = sem("h_stored")
        s_diag = sem("diag_ready")
        s_base = sem("base_ready")
        s_tr = sem("transposed")
        s_trc = sem("transposed_copied")
        s_wTp = sem("wT_transposed")
        s_wT = sem("wT_ready")
        s_ffill = sem("shifted_rows_filled")
        s_gt = sem("first_gt_ready")
        s_gtu = sem("first_gt_used")
        s_start = sem("starts_counted")
        s_sel = sem("select_ready")
        s_selu = sem("select_used")
        s_keyread = sem("selected_read")
        s_seen = sem("seen_ready")
        s_total = sem("seen_summed")
        s_keys = sem("keys_ready")
        s_hT = sem("hT_half_transposed")
        s_hTc = sem("hT_half_copied")
        s_u = sem("node_part_ready")
        s_uc = sem("node_part_copied")
        s_go = sem("gathers_may_go")
        s_idx = sem("idx_staged")
        s_gath = [sem(f"gathered{s}") for s in range(NG_)]
        s_gtail = sem("tail_gathered")
        s_edge = [sem(f"edges_loaded{s}") for s in range(2)]
        s_eused = sem("edges_used")
        s_step = sem("step_summed")
        s_hot = sem("onehot_ready")
        s_add = sem("added")
        s_hotp = sem("group_onehots_ready")
        s_cnt = sem("group_counted")
        s_cntc = sem("counts_copied")
        s_sums = sem("superblock_summed")
        s_flag = sem("flag_ready")
        s_gidx = sem("general_idx_staged")
        s_gg = sem("general_gathered")
        s_ge = sem("general_edges")
        s_gl = sem("general_targets")
        s_g32 = sem("general_rows_whole")
        s_gh = sem("general_onehot")
        s_gm = sem("general_summed")
        s_ga = sem("general_added")
        s_fp = sem("final_product")
        s_ft = sem("final_sum")
        s_xagain = [sem(f"x_loaded_again{c}") for c in range(CHUNKS)]
        s_fo = [sem(f"final_done{a}") for a in range(2)]
        s_out = sem("out_stored")

        def node_tiles(a, t0, t1):
            return a[t0 * P:t1 * P, :].rearrange("(t p) f -> p t f", p=P)

        def full_tiles(c):
            return CT if c < CHUNKS - 1 else CT - 1

        edge_pair = edge_attr[0:FULL * BATCH, :].rearrange("(g n p k) f -> p g n (k f)", g=2, p=P, k=K)
        edge_full = edge_attr[0:FULL * BATCH, :].rearrange("(n p k) f -> p n (k f)", p=P, k=K)
        edge_tail = edge_attr[FULL * BATCH:edges, :]

        def final_bank(c, a):
            return (cnt, half)[c % 2][a]

        def step_of(m, st):
            return m * BODY + (PRE + st)

        def adds_before(m):
            return 2 * (PRE - 1) if isinstance(m, int) and m == 0 else m * (2 * BODY + 4) + (2 * (PRE - 1) - 4)

        def adds_after(m, st):
            blocks = 0 if (isinstance(m, int) and m == 0) or st < 0 else 2 * (1 + (st >= SB_STEPS))
            return adds_before(m) + (2 * (st + 1) + blocks)

        ADDS = adds_before(BODIES) + 2 + 1 + 4

        block = ctx.enter_context(nc.Block())

        @block.sync
        def _(sp):
            for o, (a, v) in enumerate(((2, dst), (0, src))):
                sp.dma_start(rows_i[:, a, :], v[0:P * BATCH].rearrange("(n e) -> n e", e=BATCH)).then_inc(s_rows[o], 16)
                sp.dma_start(rows_i[0:ROWS2 - 1, a + 1, :],
                             v[P * BATCH:FULL * BATCH].rearrange("(n e) -> n e", e=BATCH)).then_inc(s_rows[o], 16)
                sp.dma_start(rows_i[ROWS2 - 1:ROWS2, a + 1, 0:TAIL],
                             v[FULL * BATCH:edges].rearrange("(n e) -> n e", n=1)).then_inc(s_rows[o], 16)
                sp.dma_start(rows_i[ROWS2 - 1:ROWS2, a + 1, TAIL:BATCH],
                             v[(FULL - 1) * BATCH + TAIL:FULL * BATCH].rearrange("(n e) -> n e", n=1)).then_inc(s_rows[o], 16)
                if o == 1:
                    for c in range(2, CHUNKS):
                        sp.dma_start(hx[:, c * CT:c * CT + full_tiles(c), :],
                                     node_tiles(x, c * CT, c * CT + full_tiles(c))).then_inc(s_x[c], 16)
                    sp.wait_ge(s_xpad, 1)
                    sp.dma_start(hx[0:LAST, TILES - 1, :], x[(TILES - 1) * P:nodes, :]).then_inc(s_x[CHUNKS - 1], 16)
            sp.dma_start(w_sb[:, :, :].rearrange("o c f -> o (c f)"), w).then_inc(s_w, 16)
            sp.dma_start(b_all[:, :], bass.AP(b.tensor, b.offset, [[0, P], [1, P]])).then_inc(s_b, 16)
            sp.wait_ge(s_ffill, 1)
            for a, v in ((1, dst), (0, src)):
                sp.dma_start(uv_i[:, a, 0:UC - 1, :],
                             bass.AP(v.tensor, v.offset, [[SHIFT, P], [SHIFT * P, UC - 1], [1, P]])).then_inc(s_uv, 16)
                sp.dma_start(uv_i[0:ULAST, a, UC - 1, :],
                             bass.AP(v.tensor, v.offset + SHIFT * P * (UC - 1), [[SHIFT, ULAST], [1, P]])).then_inc(s_uv, 16)
            for a, v in ((0, src), (1, dst)):
                sp.dma_start(tail_i[0:TAIL, a:a + 1], v[FULL * BATCH:edges].rearrange("(e o) -> e o", o=1)).then_inc(s_tail_i, 16)

            def load_edges(i, slot):
                sp.dma_start(edge_rows[:, slot, :, :, :].rearrange("p g k f -> p g (k f)"),
                             edge_pair[:, :, bass.ds(i, 1), :].rearrange("p g o e -> p g (o e)")).then_inc(s_edge[slot], 16)

            for i in range(2):
                load_edges(i, i % 2)
            for c in range(CHUNKS):
                sp.wait_ge(s_lo, c + 1)
                t0, t1 = c * CT, c * CT + full_tiles(c)
                sp.dma_start(node_tiles(h_dram, t0, t1),
                             h16[:, t0:t1, :, :].rearrange("p t a f -> p t (a f)")).then_inc(s_hstored, 16)
            sp.dma_start(h_dram[(TILES - 1) * P:nodes, :],
                         h16[0:LAST, TILES - 1, :, :].rearrange("p a f -> p (a f)")).then_inc(s_hstored, 16)
            for i in range(2, PRE):
                sp.wait_ge(s_eused, i - 1)
                load_edges(i, i % 2)
            with sp.Fori(0, BODIES) as m:
                for st in range(BODY):
                    i = step_of(m, st)
                    sp.wait_ge(s_eused, i - 1)
                    load_edges(i, (PRE + st) % 2)
            sp.wait_ge(s_eused, HALF - 1)
            sp.dma_start(edge_rows[0:TAIL, HALF % 2, 0, 0, :], edge_tail).then_inc(s_edge[HALF % 2], 16)

            sp.wait_ge(s_flag, 1)
            flag = sp.value_load(flag_i[0:1, 0:1], min_val=0, max_val=1)
            with sp.If(flag != 0):
                with sp.Fori(0, FULL) as n:
                    sp.wait_ge(s_ga, n * NWIDE + 1)
                    sp.dma_start(edge_rows[:, 0, 0, :, :].rearrange("p k f -> p (k f)"),
                                 edge_full[:, bass.ds(n, 1), :].rearrange("p o e -> p (o e)")).then_inc(s_ge, 16)
                sp.wait_ge(s_ga, FULL * NWIDE + 1)
                sp.dma_start(edge_rows[0:TAIL, 0, 0, 0, :], edge_tail).then_inc(s_ge, 16)

            for c in range(CHUNKS):
                for a in range(2):
                    sp.wait_ge(s_fo[a], c + 1)
                t0, t1 = c * CT, c * CT + full_tiles(c)
                sp.dma_start(node_tiles(out, t0, t1), hx[:, t0:t1, :]).then_inc(s_out, 16)
            sp.dma_start(out[(TILES - 1) * P:nodes, :], hx[0:LAST, TILES - 1, :]).then_inc(s_out, 16)
            sp.wait_ge(s_out, 16 * (CHUNKS + 1))

        @block.gpsimd
        def _(pool):
            pool.memset(ident[:, :], 0.0).then_inc(s_zero, 1)
            pool.memset(ones[:, :], 1.0).then_inc(s_const, 1)
            pool.wait_ge(s_zero, 1)
            pool.affine_select(out=ident[:, :], in_=ident[:, :], compare_op=ALU.not_equal, fill=1.0, base=0,
                               pattern=[[-1, P]], channel_multiplier=1).then_inc(s_const, 1)
            pool.iota(iota_i[:, :], pattern=[[1, 512]], base=0, channel_multiplier=0).then_inc(s_iota, 1)
            pool.iota(part_i[:, :], pattern=[[0, 1]], base=0, channel_multiplier=1).then_inc(s_iota, 1)
            pool.memset(ones16[:, :], 1.0).then_inc(s_const, 1)
            pool.wait_ge(s_rows[1], 16 * 4)
            for z in range(2):
                n = (P, ROWS2)[z]
                pool.tensor_copy(out=rows[0:n, z, :], in_=rows_i[0:n, z, :]).then_inc(s_rowsf[1], 1)
            pool.memset(agg[:, :, :], 0.0).then_inc(s_const, 1)
            pool.wait_ge(s_tr, 2)
            for n, v in enumerate((1, 0)):
                pool.wait_ge(s_low_i, n + 1)
                pool.tensor_copy(out=parts[:, 2 * v + 1, :, :], in_=uv_i[:, v, :, :]).then_inc(s_lparts, 1)

            def gather(rows_, dest, index, done):
                pool.indirect_dma_start(out=dest, out_offset=None, in_=h_dram,
                                        in_offset=bass.IndirectOffsetOnAxis(ap=index, axis=0)).then_inc(done, 16)

            def gather_batch(slot, done):
                for k in range(K):
                    gather(P, gathered[:, slot, k, :, :].rearrange("p a f -> p (a f)"), idx_now[:, slot, k:k + 1], done)

            pool.wait_ge(s_hstored, 16 * (CHUNKS + 1))
            for i in range(PRE):
                pool.wait_ge(s_idx, i + 1)
                gather_batch(i % NG_, s_gath[i % NG_])
            with pool.Fori(0, BODIES) as m:
                for st in range(BODY):
                    pool.wait_ge(s_idx, step_of(m, st) + 1)
                    pool.sem_inc(s_go, 1)
                    gather_batch((PRE + st) % NG_, s_gath[(PRE + st) % NG_])
            pool.wait_ge(s_tail_i, 32)
            pool.wait_ge(s_step, HALF - NG_ + 1)
            gather(TAIL, gathered[0:TAIL, HALF % NG_, 0, :, :].rearrange("p a f -> p (a f)"), tail_i[0:TAIL, 0:1], s_gtail)

            pool.wait_ge(s_flag, 1)
            flag = pool.value_load(flag_i[0:1, 0:1], min_val=0, max_val=1)
            with pool.If(flag != 0):
                with pool.Fori(0, FULL) as n:
                    pool.wait_ge(s_gidx, n + 1)
                    pool.sem_inc(s_go, 1)
                    gather_batch(0, s_gg)
                pool.wait_ge(s_ga, FULL * NWIDE + 1)
                gather(TAIL, gathered[0:TAIL, 0, 0, :, :].rearrange("p a f -> p (a f)"), tail_i[0:TAIL, 0:1], s_gg)

        @block.scalar
        def _(act):
            for c in range(2):
                act.dma_start(hx[:, c * CT:(c + 1) * CT, :], node_tiles(x, c * CT, (c + 1) * CT)).then_inc(s_x[c], 16)

            def deviation(c):
                t = slice(c * CT, (c + 1) * CT)
                act.wait_ge(s_var, c + 1)
                nc.scalar.activation(std[:, t], mv[:, t, 1], ACT.Sqrt, bias=eps[:, :]).then_inc(s_std, 1)

            def h_of(c):
                act.wait_ge(s_norm, c + 1)
                for t in range(c * CT, (c + 1) * CT):
                    last = nc.scalar.activation(hx[:, t, :], hx[:, t, :], ACT.Relu, bias=shift[:, t:t + 1],
                                                scale=rstd[:, t:t + 1])
                last.then_inc(s_h, 1)
                act.wait_ge(s_h, c + 1)
                nc.scalar.copy(h16[:, c * CT:(c + 1) * CT, 0, :], hx[:, c * CT:(c + 1) * CT, :]).then_inc(s_hi, 1)

            def low_part(c):
                act.wait_ge(s_rest, c + 1)
                nc.scalar.activation(h16[:, c * CT:(c + 1) * CT, 1, :],
                                     h_rest[:, c % 2, :].rearrange("p (t f) -> p t f", t=CT),
                                     ACT.Copy, scale=LO_SCALE).then_inc(s_lo, 1)

            def copy_hT(c):
                for a, (t0, t1) in enumerate(HALVES):
                    n = (t1 - t0) * P
                    act.wait_ge(s_hT, 2 * c + a + 1)
                    nc.scalar.copy(hT[:, a, 0:n], half[a][:, 0:n]).then_inc(s_hTc, 1)

            def stage(i, slot):
                nc.scalar.copy(idx_now[:, slot, :],
                               idx[:, :, bass.ds(i + HALF, 1)].rearrange("p k o -> p (k o)")).then_inc(s_idx, 1)

            def half_onehots(i, slot):
                act.wait_ge(s_hot, i + 1)
                nc.scalar.copy(onehot16[:, slot, 0, :, :], onehot[:, slot, 1, :, :])
                nc.scalar.activation(onehot16[:, slot, 1, :, :], onehot[:, slot, 1, :, :], ACT.Copy,
                                     scale=1.0 / LO_SCALE).then_inc(s_hot16, 1)

            act.wait_ge(s_rows[0], 16 * 4)
            for z in range(2):
                n = (P, ROWS2)[z]
                nc.scalar.copy(rows[0:n, 2 + z, :], rows_i[0:n, 2 + z, :]).then_inc(s_rowsf[0], 1)
            deviation(0)
            for c in range(CHUNKS + 1):
                if c + 1 < CHUNKS:
                    deviation(c + 1)
                if c == 2:
                    act.wait_ge(s_tr, 2)
                    for bank, (k0, k1) in zip(spread, ((0, 3), (3, K))):
                        nc.scalar.copy(idx[:, k0:k1, :], bank[0][:, 0:(k1 - k0) * NB].rearrange("p (k n) -> p k n", n=NB)
                                       ).then_inc(s_idxc, 1)
                    act.wait_ge(s_idxc, 2)
                    for i in range(PRE + 1):
                        stage(i, i % NG_)
                if c < CHUNKS:
                    h_of(c)
                if c >= 1:
                    low_part(c - 1)
                if c == 1:
                    act.wait_ge(s_wTp, 1)
                    nc.scalar.copy(wT[:, :, :].rearrange("f c o -> f (c o)"), half[1][:, 0:3 * P]).then_inc(s_wT, 1)
                if c == CHUNKS:
                    for i in range(2):
                        half_onehots(i, i)
                if 1 <= c < CHUNKS - 1:
                    copy_hT(c - 1)
                elif c == CHUNKS:
                    copy_hT(c - 2)
                if c in (2, 4):
                    v = int(c == 2)
                    act.wait_ge(s_half_i, 2 - v)
                    nc.scalar.copy(parts[:, 2 * v, :, :], half_i).then_inc(s_parts, 1)

            half_onehots(2, 0)

            def act_step(m, st):
                i, slot = step_of(m, st), st // SB_STEPS
                first_body = isinstance(m, int) and m == 0
                act.wait_ge(s_step, i + 2 - NG_)
                stage(i + 1, (PRE + st + 1) % NG_)
                if st % SB_STEPS == 0 and not first_body:
                    act.wait_ge(s_sums, 2 * m + slot - 1)
                for r in range(GPS):
                    n = GPS * (st % SB_STEPS) + r
                    act.wait_ge(s_cnt, m * (BODY * GPS) + (GPS * st + r + 1))
                    nc.scalar.copy(counts[slot][:, :, n * GN:(n + 1) * GN],
                                   cnt[r % 2][:, 0:CW].rearrange("p (a d) -> p a d", d=GN)).then_inc(s_cntc, 1)
                half_onehots(i, (PRE + st) % 2)

            for st in range(BODY):
                act_step(0, st)
            with act.Fori(1, BODIES) as m:
                for st in range(BODY):
                    act_step(m, st)

            copy_hT(CHUNKS - 1)
            act.wait_ge(s_sums, SBS)
            for c in range(CHUNKS):
                t0, t1 = c * CT, c * CT + full_tiles(c)
                act.dma_start(x_again[:, t0:t1, :], node_tiles(x, t0, t1)).then_inc(s_xagain[c], 16)
            act.dma_start(x_again[0:LAST, TILES - 1, :], x[(TILES - 1) * P:nodes, :]).then_inc(s_xagain[CHUNKS - 1], 16)

            act.wait_ge(s_flag, 1)
            flag = act.value_load(flag_i[0:1, 0:1], min_val=0, max_val=1)
            with act.If(flag != 0):
                with act.Fori(0, FULL) as n:
                    act.wait_ge(s_ga, n * NWIDE + 1)
                    nc.scalar.copy(idx_now[:, 0, :], idx[:, :, bass.ds(n, 1)].rearrange("p k o -> p (k o)")).then_inc(s_gidx, 1)

        @block.vector
        def _(dve):
            steps = [0]

            def then(ins):
                steps[0] += 1
                ins.then_inc(s_dve, 1)
                dve.wait_ge(s_dve, steps[0])

            nc.vector.memset(hx[:, TILES - 1, :], 0.0).then_inc(s_xpad, 1)
            nc.vector.memset(uv_i[:, :, UC - 1, :], 0).then_inc(s_ffill, 1)
            then(nc.vector.memset(eps[:, :], EPS))

            def node_part(c):
                for a, (t0, t1) in enumerate(HALVES):
                    dve.wait_ge(s_u, 2 * c + a + 1)
                    nc.vector.tensor_tensor(hx[:, c * CT + t0:c * CT + t1, :],
                                            half[a][:, 0:(t1 - t0) * P].rearrange("p (t f) -> p t f", f=P),
                                            b_all[:, :].unsqueeze(1).broadcast_to([P, t1 - t0, P]),
                                            ALU.add).then_inc(s_uc, 1)

            def make_onehot(i, slot):
                for g in range(2):
                    last = nc.vector.tensor_tensor(onehot[:, slot, g, :, :],
                                                   rel[:, :, bass.ds(i + g * HALF, 1)].broadcast_to([P, K, WIN]),
                                                   iota[:, 0:WIN].unsqueeze(1).broadcast_to([P, K, WIN]), ALU.is_equal)
                last.then_inc(s_hot, 1)

            def find_windows():
                dve.wait_ge(s_rowsf[0], 2)
                nr = (P, ROWS2)
                for a in range(2):
                    nc.vector.tensor_reduce(lo[0:nr[a], a:a + 1], rows[0:nr[a], 2 + a, :], AX, ALU.min)
                    last = nc.vector.tensor_reduce(hi[0:nr[a], a:a + 1], rows[0:nr[a], 2 + a, :], AX, ALU.max)
                then(last)
                dve.wait_ge(s_const, 3)
                for a in range(2):
                    nc.vector.tensor_scalar(diag[0:nr[a], a, 0:nr[a]], ident[0:nr[a], 0:nr[a]], lo[0:nr[a], a:a + 1], None,
                                            ALU.mult)
                    last = nc.vector.tensor_tensor(hi[0:nr[a], a:a + 1], hi[0:nr[a], a:a + 1], lo[0:nr[a], a:a + 1],
                                                   ALU.subtract)
                then(last)
                for a in range(2):
                    last = nc.vector.tensor_scalar(wide_span[0:nr[a], a:a + 1], hi[0:nr[a], a:a + 1], float(WIN), None, ALU.is_ge)
                last.then_inc(s_diag, 1)

            def use_windows():
                dve.wait_ge(s_base, 1)
                nc.vector.tensor_copy(base[:, :], half[0][:, 0:NB])
                nc.vector.tensor_copy(base_i[0:1, :], half[0][0:1, 0:NB])
                then(nc.vector.tensor_copy(flag_w[0:1, 0:1], half[0][0:1, NB:NB + 1]))
                dve.wait_ge(s_tr, 1)
                for bank, (k0, k1) in zip(spread, ((0, 3), (3, K))):
                    nc.vector.tensor_tensor(rel[:, k0:k1, :], bank[1][:, 0:(k1 - k0) * NB].rearrange("p (k n) -> p k n", n=NB),
                                            base[:, :].unsqueeze(1).broadcast_to([P, k1 - k0, NB]),
                                            ALU.subtract).then_inc(s_trc, 1)
                dve.wait_ge(s_trc, 2)
                dve.wait_ge(s_tail_i, 32)
                nc.vector.tensor_tensor(tail_rel[0:TAIL, :], tail_i[0:TAIL, 1:2], base[0:TAIL, FULL:NB], ALU.subtract)

                for i in range(2):
                    make_onehot(i, i)

            def prepare_starts():
                dve.wait_ge(s_uv, 64)
                nc.vector.tensor_copy(row0[:, :], uv_i[:, 1, :, 0])
                nc.vector.tensor_scalar(first[:, :], iota[:, 0:GROUPS], float(GN), None, ALU.mult)
                then(nc.vector.tensor_scalar(part32[:, :], part[:, :], float(SHIFT), None, ALU.mult))
                then(nc.vector.tensor_scalar(beyond[:, :], iota[:, 0:P], part32[:, 0:1],
                                             float(COUNTED - SHIFT * P * (UC - 1)), ALU.add, ALU.is_ge))
                then(nc.vector.scalar_tensor_tensor(out=row0[:, UC - 1:UC], in0=beyond[:, 0:1], scalar=BIG,
                                                    in1=row0[:, UC - 1:UC], op0=ALU.mult, op1=ALU.add))

            def find_starts():
                for c in range(UC):
                    if c >= NSEL:
                        dve.wait_ge(s_gtu, c + 1 - NSEL)
                    nc.vector.tensor_scalar(first_gt[:, c % NSEL, :], first[:, :], row0[:, c:c + 1], None,
                                            ALU.is_gt).then_inc(s_gt, 1)

            def split_edges(v):
                dve.wait_ge(s_uv, 64)
                if v == 0:
                    dve.wait_ge(s_parts, 1)
                nc.vector.tensor_scalar(half_i, uv_i[:, v, :, :], 7, None, ALU.arith_shift_right).then_inc(s_half_i, 1)
                dve.wait_ge(s_half_i, 2 - v)
                nc.vector.tensor_scalar(uv_i[:, v, :, :], uv_i[:, v, :, :], P - 1, None,
                                        ALU.bitwise_and).then_inc(s_low_i, 1)

            def add_window(n, slot, col, before):
                at = dve.value_load(base_i[0:1, bass.ds(n, 1)], min_val=0, max_val=nodes - 1)
                dve.wait_ge(s_add, before)
                a = 2 if col else 1
                nc.vector.tensor_tensor(agg[:, 0:a, bass.ds(at, WIN)], agg[:, 0:a, bass.ds(at, WIN)],
                                        acc[slot][:, col:col + a * WIN].rearrange("p (a w) -> p a w", a=a),
                                        ALU.add).then_inc(s_add, 1)

            def add_step(i, slot, before):
                dve.wait_ge(s_step, i + 1)
                add_window(i, slot, 0, before)
                add_window(i + HALF, slot, WIN, before + 1)

            def add_superblock(n, slot, before):
                dve.wait_ge(s_sums, n + 1)
                dve.wait_ge(s_add, before)
                at = agg[:, 1, bass.ds(n * SBN, SBN)]
                nc.vector.scalar_tensor_tensor(out=at, in0=sums[slot][:, SBN:2 * SBN], scalar=1.0 / LO_SCALE, in1=at,
                                               op0=ALU.mult, op1=ALU.add).then_inc(s_add, 1)
                dve.wait_ge(s_add, before + 1)
                nc.vector.tensor_tensor(at, at, sums[slot][:, 0:SBN], ALU.add).then_inc(s_add, 1)

            def place_groups():
                dve.wait_ge(s_start, 1)
                t_start = t_a[:, :, :].rearrange("p j g -> p (j g)")
                then(nc.vector.tensor_scalar(t_start, sums[0][:, 0:GROUPS], -1.0, 0.0, ALU.add, ALU.max))
                for j in range(2):
                    last = nc.vector.tensor_scalar(start[:, j, :], t_start, part[:, 0:1], float(j * P // SHIFT),
                                                   ALU.subtract, ALU.add)
                then(last)
                dve.wait_ge(s_parts, 2)
                dve.wait_ge(s_lparts, 2)
                then(nc.vector.scalar_tensor_tensor(out=parts[:, 2, UC - 1, :], in0=beyond[:, :], scalar=float(P),
                                                    in1=parts[:, 2, UC - 1, :], op0=ALU.mult, op1=ALU.add))

            def select_edges(hh, c0, c1):
                g = slice(hh * GH, (hh + 1) * GH)
                for c in range(c0, c1):
                    n = hh * UC + c
                    if n >= NSEL:
                        dve.wait_ge(s_selu, n + 1 - NSEL)
                    nc.vector.tensor_scalar(select[:, n % NSEL, :, :], start[:, :, g], float(c * P), None,
                                            ALU.is_equal).then_inc(s_sel, 1)

            def make_keys(hh):
                g = slice(hh * GH, (hh + 1) * GH)
                dve.wait_ge(s_selu, (hh + 1) * UC)
                tile_, lane_, dhi, dlo = (z[:, 0:2 * GH].rearrange("p (j g) -> p j g", j=2) for z in chosen)
                nc.vector.tensor_copy(lane[:, :, g], lane_)
                nc.vector.tensor_copy(t_b[:, :, :], dlo)
                then(nc.vector.tensor_copy(key[:, :, g], tile_))
                nc.vector.scalar_tensor_tensor(out=t_a[:, :, :], in0=dhi, scalar=float(P), in1=t_b[:, :, :],
                                               op0=ALU.mult, op1=ALU.add).then_inc(s_keyread, 1)
                dve.wait_ge(s_keyread, hh + 1)
                then(nc.vector.tensor_tensor(t_a[:, :, :], t_a[:, :, :],
                                             first[:, g].unsqueeze(1).broadcast_to([P, 2, GH]), ALU.subtract))
                then(nc.vector.tensor_scalar(t_b[:, :, :], t_a[:, :, :], 0.0, None, ALU.is_ge))
                then(nc.vector.scalar_tensor_tensor(out=t_b[:, :, :], in0=t_a[:, :, :], scalar=float(GN - 1),
                                                    in1=t_b[:, :, :], op0=ALU.is_le, op1=ALU.mult))
                then(nc.vector.tensor_reduce(seen[:, hh:hh + 1], t_b[:, :, :].rearrange("p j g -> p (j g)"), AX, ALU.add))
                then(nc.vector.scalar_tensor_tensor(out=t_a[:, :, :], in0=key[:, :, g], scalar=float(GN),
                                                    in1=t_a[:, :, :], op0=ALU.mult, op1=ALU.add))
                then(nc.vector.scalar_tensor_tensor(out=t_a[:, :, :], in0=t_a[:, :, :], scalar=1.0,
                                                    in1=t_b[:, :, :], op0=ALU.add, op1=ALU.mult))
                nc.vector.tensor_scalar(key[:, :, g], t_a[:, :, :], -1.0, None, ALU.add).then_inc(s_keys, 1)

            dve.wait_ge(s_iota, 2)
            nc.vector.tensor_copy(iota[:, :], iota_i[:, :])
            nc.vector.tensor_copy(iota16[:, :], iota_i[:, :])
            then(nc.vector.tensor_copy(part[:, :], part_i[:, :]))
            for c in range(CHUNKS + 2):
                if c < CHUNKS:
                    dve.wait_ge(s_x[c], 16 if c < CHUNKS - 1 else 32)
                    for t in range(CT):
                        last = nc.vector.bn_stats(stats[:, t, :], hx[:, c * CT + t, :])
                    then(last)
                    for t in range(CT):
                        last = nc.vector.bn_aggr(mv[:, c * CT + t, :], stats[:, t, :])
                    last.then_inc(s_var, 1)
                    dve.wait_ge(s_var, c + 1)
                if 1 <= c <= CHUNKS:
                    t = slice((c - 1) * CT, c * CT)
                    dve.wait_ge(s_std, c)
                    then(nc.vector.reciprocal(rstd[:, t], std[:, t]))
                    nc.vector.scalar_tensor_tensor(out=shift[:, t], in0=mv[:, t, 0], scalar=-1.0, in1=rstd[:, t],
                                                   op0=ALU.mult, op1=ALU.mult).then_inc(s_norm, 1)
                if c >= 2:
                    n = c - 2
                    dve.wait_ge(s_hi, n + 1)
                    if n >= 2:
                        dve.wait_ge(s_lo, n - 1)
                    nc.vector.scalar_tensor_tensor(
                        out=h_rest[:, n % 2, :].rearrange("p (t f) -> p t f", t=CT),
                        in0=h16[:, n * CT:(n + 1) * CT, 0, :], scalar=-1.0, in1=hx[:, n * CT:(n + 1) * CT, :],
                        op0=ALU.mult, op1=ALU.add).then_inc(s_rest, 1)
                if 3 <= c < CHUNKS + 1:
                    node_part(c - 3)
                if c == 1:
                    find_windows()
                if c == 2:
                    use_windows()
                    dve.wait_ge(s_b, 16)
                if c == 3:
                    prepare_starts()
                    split_edges(1)
                if c == 4:
                    find_starts()
                if c == 5:
                    split_edges(0)
                if c == 6:
                    place_groups()
                    select_edges(0, 0, NSEL)
            select_edges(0, NSEL, UC)
            make_keys(0)
            select_edges(1, 0, NSEL)
            node_part(CHUNKS - 2)
            dve.wait_ge(s_const, 4)
            add_step(0, 0, 0)
            make_onehot(2, 0)
            select_edges(1, NSEL, UC)
            make_keys(1)

            def group_onehots(m, st):
                for r in range(GPS):
                    g = m * (BODY * GPS) + (GPS * st + r)
                    if not (isinstance(m, int) and m + st == 0):
                        dve.wait_ge(s_cnt, g + (1 - GPS))
                    for j in range(2):
                        nc.vector.tensor_scalar(hot_key[:, r, j, :], iota16[:, 0:CW], key[:, j, bass.ds(g, 1)], None,
                                                ALU.is_equal)
                        last = nc.vector.tensor_scalar(hot_lane[:, r, j, :], iota16[:, 0:P], lane[:, j, bass.ds(g, 1)],
                                                       None, ALU.is_equal)
                    last.then_inc(s_hotp, 1)

            group_onehots(0, 0)
            add_step(1, 1, 2)

            def raise_flag():
                dve.wait_ge(s_keys, 2)
                dve.wait_ge(s_total, 1)
                then(nc.vector.tensor_copy(flag_c[0:1, 0:1], sums[1][0:1, 0:1]))
                then(nc.vector.tensor_scalar(flag_c[0:1, 0:1], sums[1][0:1, 1:2], flag_c[0:1, 0:1], float(COUNTED),
                                             ALU.add, ALU.not_equal))
                then(nc.vector.tensor_tensor(flag_c[0:1, 0:1], flag_c[0:1, 0:1], flag_w[0:1, 0:1], ALU.add))
                nc.vector.tensor_scalar(flag_i[0:1, 0:1], flag_c[0:1, 0:1], 1.0, None, ALU.min).then_inc(s_flag, 1)

            def dve_step(m, st):
                i = step_of(m, st)
                first_body = isinstance(m, int) and m == 0
                before = adds_after(m, st - 1)
                if st % SB_STEPS == 0 and not first_body:
                    slot = st // SB_STEPS
                    add_superblock(2 * m + (slot - 2), slot, before)
                    before = before + 2
                if not (first_body and st == 0):
                    group_onehots(m, st)
                dve.wait_ge(s_step, i - 1)
                make_onehot(i, (PRE + st) % 2)
                add_step(i - 1, (PRE + st - 1) % 2, before)

            for st in range(BODY):
                dve_step(0, st)
                if st == 1:
                    raise_flag()
            with dve.Fori(1, BODIES) as m:
                for st in range(BODY):
                    dve_step(m, st)
            done = adds_before(BODIES)
            slot = HALF % 2
            dve.wait_ge(s_step, HALF - 1)
            nc.vector.tensor_tensor(onehot[0:TAIL, slot, 0, 0, :], tail_rel[0:TAIL, 0:1].broadcast_to([TAIL, WIN]),
                                    iota[0:TAIL, 0:WIN], ALU.is_equal).then_inc(s_hot, 1)
            dve.wait_ge(s_hot, HALF + 1)
            nc.vector.tensor_copy(onehot16[0:TAIL, slot, 0, 0, :], onehot[0:TAIL, slot, 0, 0, :])
            nc.vector.tensor_scalar(onehot16[0:TAIL, slot, 1, 0, :], onehot[0:TAIL, slot, 0, 0, :], 1.0 / LO_SCALE,
                                    None, ALU.mult).then_inc(s_hot, 1)
            add_step(HALF - 1, (HALF - 1) % 2, done)
            add_superblock(SBS - 2, SBS % 2, done + 2)
            dve.wait_ge(s_step, HALF + 1)
            add_window(FULL, slot, WIN, done + 4)
            add_superblock(SBS - 1, (SBS - 1) % 2, done + 5)

            node_part(CHUNKS - 1)

            dve.wait_ge(s_add, ADDS)
            dve.wait_ge(s_flag, 1)
            flag = dve.value_load(flag_i[0:1, 0:1], min_val=0, max_val=1)
            with dve.If(flag != 0):
                nc.vector.memset(agg[:, :, :], 0.0).then_inc(s_ga, 1)

                def wide_sums(ks, windows, targets):
                    with dve.Fori(0, NWIDE) as j:
                        dve.wait_ge(s_gl, targets)
                        nc.vector.tensor_tensor(wide_hot[:, 0:ks, :],
                                                left[:, 0:ks].unsqueeze(2).broadcast_to([P, ks, WIDE]),
                                                iota[:, 0:WIDE].unsqueeze(1).broadcast_to([P, ks, WIDE]),
                                                ALU.is_equal).then_inc(s_gh, 1)
                        dve.wait_ge(s_gh, windows + j + 1)
                        nc.vector.tensor_scalar(left[:, :], left[:, :], -float(WIDE), None, ALU.add)
                        dve.wait_ge(s_gm, windows + j + 1)
                        for a in range(2):
                            at = agg[:, a, bass.ds(j * WIDE, WIDE)]
                            last = nc.vector.tensor_tensor(at, at, cnt[a][:, 0:WIDE], ALU.add)
                        last.then_inc(s_ga, 1)
                        dve.wait_ge(s_ga, windows + j + 2)

                with dve.Fori(0, FULL) as n:
                    dve.wait_ge(s_ga, n * NWIDE + 1)
                    nc.vector.tensor_scalar(left[:, :], rel[:, :, bass.ds(n, 1)].rearrange("p k o -> p (k o)"),
                                            base[:, bass.ds(n, 1)], None, ALU.add).then_inc(s_gl, 1)
                    dve.wait_ge(s_gg, (16 * K) * n + 16 * K)
                    nc.vector.scalar_tensor_tensor(out=whole, in0=gathered[:, 0, :, 1, :], scalar=1.0 / LO_SCALE,
                                                   in1=gathered[:, 0, :, 0, :], op0=ALU.mult,
                                                   op1=ALU.add).then_inc(s_g32, 1)
                    wide_sums(K, n * NWIDE, n + 1)
                nc.vector.tensor_copy(left[0:TAIL, 0:1], tail_i[0:TAIL, 1:2]).then_inc(s_gl, 1)
                dve.wait_ge(s_gg, 16 * K * FULL + 16)
                nc.vector.scalar_tensor_tensor(out=whole[0:TAIL, 0, :], in0=gathered[0:TAIL, 0, 0, 1, :],
                                               scalar=1.0 / LO_SCALE, in1=gathered[0:TAIL, 0, 0, 0, :], op0=ALU.mult,
                                               op1=ALU.add).then_inc(s_g32, 1)
                wide_sums(1, FULL * NWIDE, FULL + 1)

            for c in range(CHUNKS):
                dve.wait_ge(s_xagain[c], 16 if c < CHUNKS - 1 else 32)
                for a, (t0, t1) in enumerate(HALVES):
                    n = (t1 - t0) * P
                    o = hx[:, CT * c + t0:CT * c + t1, :].rearrange("p t f -> p (t f)")
                    xs = x_again[:, CT * c + t0:CT * c + t1, :].rearrange("p t f -> p (t f)")
                    dve.wait_ge(s_fp, 2 * c + a + 1)
                    nc.vector.tensor_tensor(o, o, final_bank(c, a)[:, 0:n], ALU.add).then_inc(s_ft, 1)
                    dve.wait_ge(s_ft, 2 * c + a + 1)
                    nc.vector.scalar_tensor_tensor(out=o, in0=o, scalar=0.0, in1=xs, op0=ALU.max,
                                                   op1=ALU.add).then_inc(s_fo[a], 1)

        @block.tensor
        def _(pe):
            nr = (P, ROWS2)
            pe.wait_ge(s_const, 3)
            for o, v in enumerate((1, 0)):
                pe.wait_ge(s_rowsf[o], 2)
                for bank, (k0, k1) in zip(spread, ((0, 3), (3, K))):
                    for k in range(k0, k1):
                        for a in range(2):
                            c0 = (k - k0) * NB + a * P
                            last = nc.tensor.transpose(
                                bank[v][:, c0:c0 + nr[a]],
                                rows[0:nr[a], 2 * v + a, :].rearrange("n (p k) -> n k p", k=K)[:, k, :],
                                ident[0:nr[a], 0:nr[a]])
                last.then_inc(s_tr, 1)
                if o == 0:
                    pe.wait_ge(s_diag, 1)
                    for a in range(2):
                        nc.tensor.matmul(half[0][:, a * P:a * P + nr[a]], ones[0:nr[a], :], diag[0:nr[a], a, 0:nr[a]],
                                         start=True, stop=True)
                    nc.tensor.matmul(half[0][:, NB:NB + 1], ones[:, :], wide_span[:, 0:1], start=True, stop=False)
                    nc.tensor.matmul(half[0][:, NB:NB + 1], ones[0:ROWS2, :], wide_span[0:ROWS2, 1:2], start=False,
                                     stop=True).then_inc(s_base, 1)
            pe.wait_ge(s_w, 16)
            for c in range(3):
                last = nc.tensor.transpose(half[1][:, c * P:(c + 1) * P], w_sb[:, c, :], ident[:, :])
            last.then_inc(s_wTp, 1)
            def products(out_, rows_, left_, right):
                for k in range(len(left_)):
                    last = nc.tensor.matmul(out_, left_[k][0:rows_], right[k][0:rows_], start=(k == 0),
                                            stop=(k == len(left_) - 1))
                return last

            def by_k(v):
                return [v[:, k, :] for k in range(K)]

            def choose(hh):
                if hh:
                    pe.wait_ge(s_keyread, 1)
                for c in range(UC):
                    pe.wait_ge(s_sel, hh * UC + c + 1)
                    for v in range(4):
                        last = nc.tensor.matmul(chosen[v][:, 0:2 * GH], parts[:, v, c, :],
                                                select[:, (hh * UC + c) % NSEL, :, :].rearrange("p j g -> p (j g)"),
                                                start=(c == 0), stop=(c == UC - 1))
                    last.then_inc(s_selu, 1)
            def sum_step(i, slot, gslot, fill, gfill):
                pe.wait_ge(s_edge[slot], 16 * fill + 16)
                pe.wait_ge(s_hot, i + 1)
                for g in range(2):
                    last = products(acc[slot][:, g * WIN:(g + 1) * WIN], P, by_k(edge_rows[:, slot, g, :, :]),
                                    by_k(onehot[:, slot, g, :, :]))
                last.then_inc(s_eused, 1)
                pe.wait_ge(s_gath[gslot], (16 * K) * gfill + 16 * K)
                pe.wait_ge(s_hot16, i + 1)
                products(acc[slot][:, 2 * WIN:3 * WIN], P,
                         [gathered[:, gslot, k, a, :] for k in range(K) for a in range(2)],
                         [onehot16[:, slot, a, k, :] for k in range(K) for a in range(2)]).then_inc(s_step, 1)

            def transpose_h(c):
                pe.wait_ge(s_h, c + 1)
                for a, (t0, t1) in enumerate(HALVES):
                    if c:
                        pe.wait_ge(s_uc, 2 * c + a - 1)
                    for t in range(t0, t1):
                        last = nc.tensor.transpose(half[a][:, (t - t0) * P:(t - t0 + 1) * P], hx[:, c * CT + t, :],
                                                   ident[:, :])
                    last.then_inc(s_hT, 1)

            def node_products(c):
                for a, (t0, t1) in enumerate(HALVES):
                    pe.wait_ge(s_hTc, 2 * c + a + 1)
                    for t in range(t1 - t0):
                        o = slice(t * P, (t + 1) * P)
                        last = nc.tensor.matmul(half[a][:, o], hT[:, a, o], wT[:, 0, :], start=True, stop=True)
                    last.then_inc(s_u, 1)

            pe.wait_ge(s_trc, 1)
            pe.wait_ge(s_wT, 1)
            for c in range(CHUNKS - 1):
                transpose_h(c)
                node_products(c)
                if c == 1:
                    pe.wait_ge(s_idxc, 2)
                    pe.wait_ge(s_trc, 2)
                    for n in range(UC):
                        pe.wait_ge(s_gt, n + 1)
                        last = nc.tensor.matmul(sums[0][:, 0:GROUPS], ones16[:, :], first_gt[:, n % NSEL, :],
                                                start=(n == 0), stop=(n == UC - 1))
                        last.then_inc(s_gtu if n < UC - 1 else s_start, 1)
                if c == 4:
                    choose(0)

            sum_step(0, 0, 0, 0, 0)
            choose(1)
            sum_step(1, 1, 1, 0, 0)
            pe.wait_ge(s_add, 2)
            sum_step(2, 0, 2, 1, 0)
            pe.wait_ge(s_keys, 2)
            nc.tensor.matmul(sums[1][:, 0:2], ones[:, :], seen[:, :], start=True, stop=True).then_inc(s_total, 1)

            pe.wait_ge(s_lo, CHUNKS)

            def sum_superblock(slot, part, a0, a1):
                for a in range(a0, a1):
                    last = nc.tensor.matmul(sums[slot][:, part * SBN:(part + 1) * SBN], h16[:, a, part, :],
                                            counts[slot][:, a, :], start=(a == 0), stop=(a == TILES - 1))
                return last

            QUARTERS = [(0, 0, (TILES + 1) // 2), (0, (TILES + 1) // 2, TILES),
                        (1, 0, (TILES + 1) // 2), (1, (TILES + 1) // 2, TILES)]

            def pe_step(m, st):
                i = step_of(m, st)
                first_body = isinstance(m, int) and m == 0

                def count(groups):
                    for r in groups:
                        g = m * (BODY * GPS) + (GPS * st + r)
                        pe.wait_ge(s_hotp, g + 1)
                        if not (first_body and st == 0 and r < 2):
                            pe.wait_ge(s_cntc, g - 1)
                        for j in range(2):
                            last = nc.tensor.matmul(cnt[r % 2][:, 0:CW], hot_lane[:, r, j, :], hot_key[:, r, j, :],
                                                    start=(j == 0), stop=(j == 1))
                        last.then_inc(s_cnt, 1)

                count((0, 1))
                later, quarter = divmod(st, SB_STEPS)
                if later or not first_body:
                    slot = 1 - later
                    if quarter == 0:
                        pe.wait_ge(s_cntc, m * (2 * SB_GROUPS) + SB_GROUPS * later)
                        if not first_body:
                            pe.wait_ge(s_add, adds_after(m, 0) - 2 if later else m * (2 * BODY + 4) - BODY)
                    last = sum_superblock(slot, *QUARTERS[quarter])
                    if quarter == SB_STEPS - 1:
                        last.then_inc(s_sums, 1)
                count((2, 3))
                pe.wait_ge(s_add, adds_after(m, st - 1))
                sum_step(i, (PRE + st) % 2, (PRE + st) % NG_, m * (BODY // 2) + (PRE + st) // 2,
                         m * (BODY // NG_) + (PRE + st) // NG_)

            for st in range(BODY):
                pe_step(0, st)
            with pe.Fori(1, BODIES) as m:
                for st in range(BODY):
                    pe_step(m, st)

            slot, fill = HALF % 2, HALF // 2
            pe.wait_ge(s_edge[slot], 16 * (fill + 1))
            pe.wait_ge(s_gtail, 16)
            pe.wait_ge(s_hot, HALF + 2)
            pe.wait_ge(s_add, adds_before(BODIES))
            products(acc[slot][:, WIN:2 * WIN], TAIL, [edge_rows[:, slot, 0, 0, :]], [onehot[:, slot, 0, 0, :]])
            products(acc[slot][:, 2 * WIN:3 * WIN], TAIL, [gathered[:, HALF % NG_, 0, a, :] for a in range(2)],
                     [onehot16[:, slot, a, 0, :] for a in range(2)]).then_inc(s_step, 1)
            transpose_h(CHUNKS - 1)
            slot = (SBS - 1) % 2
            pe.wait_ge(s_cntc, GROUPS)
            for q in QUARTERS:
                last = sum_superblock(slot, *q)
            last.then_inc(s_sums, 1)
            node_products(CHUNKS - 1)

            pe.wait_ge(s_add, ADDS)
            flag = pe.value_load(flag_i[0:1, 0:1], min_val=0, max_val=1)
            with pe.If(flag != 0):
                def wide_products(rows_, ks, done):
                    pe.wait_ge(s_gh, done + 1)
                    pe.wait_ge(s_ga, done + 1)
                    for o, v in ((cnt[0], edge_rows[:, 0, 0, :, :]), (cnt[1], whole)):
                        last = products(o[:, 0:WIDE], rows_, by_k(v)[0:ks], by_k(wide_hot)[0:ks])
                    last.then_inc(s_gm, 1)

                with pe.Fori(0, FULL) as n:
                    with pe.Fori(0, NWIDE) as j:
                        pe.wait_ge(s_ge, 16 * n + 16)
                        pe.wait_ge(s_g32, n + 1)
                        wide_products(P, K, n * NWIDE + j)
                pe.wait_ge(s_ge, 16 * NB)
                pe.wait_ge(s_g32, NB)
                with pe.Fori(0, NWIDE) as j:
                    wide_products(TAIL, 1, FULL * NWIDE + j)
                pe.wait_ge(s_ga, NB * NWIDE + 1)

            for c in range(CHUNKS):
                for a, (t0, t1) in enumerate(HALVES):
                    if c >= 2:
                        pe.wait_ge(s_fo[a], c - 1)
                    elif c:
                        pe.wait_ge(s_uc, 2 * CHUNKS)
                    for t in range(t0, t1):
                        o = final_bank(c, a)[:, (t - t0) * P:(t - t0 + 1) * P]
                        n = slice((c * CT + t) * P, (c * CT + t + 1) * P)
                        nc.tensor.matmul(o, agg[:, 1, n], wT[:, 1, :], start=True, stop=False)
                        last = nc.tensor.matmul(o, agg[:, 0, n], wT[:, 2, :], start=False, stop=True)
                    last.then_inc(s_fp, 1)


_INS = ["x", "src", "dst", "edge_attr_128", "L0_gnn_W", "L0_gnn_b"]


def kernel(**inputs):
    import concourse.bacc as bacc
    from concourse.bass_utils import run_bass_kernel_spmd

    nc = bacc.Bacc("TRN2", target_bir_lowering=False, num_devices=1)
    arrays, args = {}, []
    for name in _INS:
        a = np.ascontiguousarray(inputs[name])
        arrays[f"in_{name}"] = a
        args.append(nc.dram_tensor(f"in_{name}", a.shape, mybir.dt.from_np(a.dtype), kind="ExternalInput").ap())
    shape = inputs["x"].shape
    args.append(nc.dram_tensor("result", shape, F32, kind="ExternalOutput").ap())
    build(nc, *args)
    r = run_bass_kernel_spmd(nc, [arrays], core_ids=[0])
    return r.results[0]["result"]
```
